# Optimizing a Trainium2 kernel written in Bass

```python
import numpy as np
import jax
import jax.numpy as jnp

def _softmax(x, axis=-1):
    return jax.nn.softmax(x, axis=axis)

def _gelu(x):
    return jax.nn.gelu(x, approximate=True)

def _silu(x):
    return jax.nn.silu(x)

def _sigmoid(x):
    return jax.nn.sigmoid(x)

def _layernorm(x, axis=-1, eps=1e-05):
    m = jnp.mean(x, axis=axis, keepdims=True)
    v = jnp.var(x, axis=axis, keepdims=True)
    return (x - m) / jnp.sqrt(v + eps)

def _scatter_add(tgt, idx, src, axis=0):
    return tgt.at[idx].add(src)

def _segment_sum(src, seg, n):
    return jax.ops.segment_sum(src, seg, n)
kernel_name = 'mk_seq_preln_d1_jaxref_r8_c86fb0'

def setup_inputs(seed: int=0):
    np.random.seed(seed)
    _w = jnp.asarray

    def _L0_attn_setup():
        import jax, jax.numpy as jnp
        import numpy as np
        NUM_HEAD = 32
        NUM_KV = 8
        HIDDEN = 512
        HEAD_DIM = HIDDEN // NUM_HEAD
        KV_DIM = HEAD_DIM * NUM_KV
        key = jax.random.key(seed)
        ks = jax.random.split(key, 5)
        bs, seq = (2, 256)
        scale = 0.02
        return {'x': jax.random.normal(ks[0], (bs, seq, HIDDEN), dtype=jnp.float32), 'w_q': jax.random.normal(ks[1], (HIDDEN, HIDDEN), dtype=jnp.float32) * scale, 'w_k': jax.random.normal(ks[2], (HIDDEN, KV_DIM), dtype=jnp.float32) * scale, 'w_v': jax.random.normal(ks[3], (HIDDEN, KV_DIM), dtype=jnp.float32) * scale, 'w_o': jax.random.normal(ks[4], (HIDDEN, HIDDEN), dtype=jnp.float32) * scale}
    _L0_attn_in = _L0_attn_setup()

    def _L0_ffn_setup():
        import jax, jax.numpy as jnp
        import numpy as np
        D_MODEL = 512
        D_HIDDEN = 1376
        RANK = 16
        BATCH, SEQ = (2, 256)

        def _matmul_lora(x, w, a, b, scale=1.0):
            out = jnp.einsum('bsd,hd->bsh', x, w)
            out = out + jnp.einsum('bsr,hr->bsh', jnp.einsum('bsd,rd->bsr', x, a), b) * scale
            return out
        key = jax.random.key(seed)
        ks = jax.random.split(key, 10)
        s = 0.02
        return {'x': jax.random.normal(ks[0], (BATCH, SEQ, D_MODEL), jnp.float32), 'gate_w': jax.random.normal(ks[1], (D_HIDDEN, D_MODEL), jnp.float32) * s, 'up_w': jax.random.normal(ks[2], (D_HIDDEN, D_MODEL), jnp.float32) * s, 'down_w': jax.random.normal(ks[3], (D_MODEL, D_HIDDEN), jnp.float32) * s, 'gate_a': jax.random.normal(ks[4], (RANK, D_MODEL), jnp.float32) * s, 'gate_b': jax.random.normal(ks[5], (D_HIDDEN, RANK), jnp.float32) * s, 'up_a': jax.random.normal(ks[6], (RANK, D_MODEL), jnp.float32) * s, 'up_b': jax.random.normal(ks[7], (D_HIDDEN, RANK), jnp.float32) * s, 'down_a': jax.random.normal(ks[8], (RANK, D_HIDDEN), jnp.float32) * s, 'down_b': jax.random.normal(ks[9], (D_MODEL, RANK), jnp.float32) * s}
    _L0_ffn_in = _L0_ffn_setup()
    _d = {'L0_attn_x': _L0_attn_in['x'], 'L0_attn_w_q': _L0_attn_in['w_q'], 'L0_attn_w_k': _L0_attn_in['w_k'], 'L0_attn_w_v': _L0_attn_in['w_v'], 'L0_attn_w_o': _L0_attn_in['w_o'], 'L0_ffn_gate_w': _L0_ffn_in['gate_w'], 'L0_ffn_up_w': _L0_ffn_in['up_w'], 'L0_ffn_down_w': _L0_ffn_in['down_w'], 'L0_ffn_gate_a': _L0_ffn_in['gate_a'], 'L0_ffn_gate_b': _L0_ffn_in['gate_b'], 'L0_ffn_up_a': _L0_ffn_in['up_a'], 'L0_ffn_up_b': _L0_ffn_in['up_b'], 'L0_ffn_down_a': _L0_ffn_in['down_a'], 'L0_ffn_down_b': _L0_ffn_in['down_b']}
    _x0 = _d['L0_attn_x']
    _d['L0_attn_x'] = jax.random.normal(jax.random.fold_in(jax.random.key(seed), 1), (2, 1024, 512), dtype=_x0.dtype)
    del _x0
    return _d

def reference(L0_attn_x, L0_attn_w_q, L0_attn_w_k, L0_attn_w_v, L0_attn_w_o, L0_ffn_gate_w, L0_ffn_up_w, L0_ffn_down_w, L0_ffn_gate_a, L0_ffn_gate_b, L0_ffn_up_a, L0_ffn_up_b, L0_ffn_down_a, L0_ffn_down_b):

    def _L0_attn_ref(x, w_q, w_k, w_v, w_o):
        import jax, jax.numpy as jnp
        import numpy as np
        NUM_HEAD = 32
        NUM_KV = 8
        HIDDEN = 512
        HEAD_DIM = HIDDEN // NUM_HEAD
        KV_DIM = HEAD_DIM * NUM_KV
        bs, seq, _ = x.shape
        group = NUM_HEAD // NUM_KV
        q = (x @ w_q).reshape(bs, seq, NUM_HEAD, HEAD_DIM).transpose(0, 2, 1, 3)
        k = (x @ w_k).reshape(bs, seq, NUM_KV, HEAD_DIM).transpose(0, 2, 1, 3)
        v = (x @ w_v).reshape(bs, seq, NUM_KV, HEAD_DIM).transpose(0, 2, 1, 3)
        k = jnp.repeat(k, group, axis=1)
        v = jnp.repeat(v, group, axis=1)
        scores = jnp.einsum('bhqd,bhkd->bhqk', q, k) / jnp.sqrt(jnp.float32(HEAD_DIM))
        weights = jax.nn.softmax(scores, axis=-1)
        o = jnp.einsum('bhqk,bhkd->bhqd', weights, v)
        o = o.transpose(0, 2, 1, 3).reshape(bs, seq, HIDDEN)
        return o @ w_o

    def _L0_ffn_ref(x, gate_w, up_w, down_w, gate_a, gate_b, up_a, up_b, down_a, down_b):
        import jax, jax.numpy as jnp
        import numpy as np
        D_MODEL = 512
        D_HIDDEN = 1376
        RANK = 16
        BATCH, SEQ = (2, 256)

        def _matmul_lora(x, w, a, b, scale=1.0):
            out = jnp.einsum('bsd,hd->bsh', x, w)
            out = out + jnp.einsum('bsr,hr->bsh', jnp.einsum('bsd,rd->bsr', x, a), b) * scale
            return out
        gate = _matmul_lora(x, gate_w, gate_a, gate_b)
        up = _matmul_lora(x, up_w, up_a, up_b)
        hidden = jax.nn.silu(gate) * up
        out = _matmul_lora(hidden, down_w, down_a, down_b)
        return out
    x = L0_attn_x
    x = x + _L0_attn_ref(_layernorm(x, axis=-1), L0_attn_w_q, L0_attn_w_k, L0_attn_w_v, L0_attn_w_o)
    x = x + _L0_ffn_ref(_layernorm(x, axis=-1), L0_ffn_gate_w, L0_ffn_up_w, L0_ffn_down_w, L0_ffn_gate_a, L0_ffn_gate_b, L0_ffn_up_a, L0_ffn_up_b, L0_ffn_down_a, L0_ffn_down_b)
    return x

_drawn_inputs = setup_inputs


def setup_inputs(seed=0):
    import zlib

    import numpy as np

    out = dict(_drawn_inputs(seed))
    spreads = {}
    factors = {'L0_attn_w_q': 8.0,
     'L0_attn_w_k': 8.0,
     'L0_attn_w_v': 8.0,
     'L0_attn_w_o': 8.0,
     'L0_ffn_gate_a': 8.0,
     'L0_ffn_gate_b': 8.0,
     'L0_ffn_up_a': 6.394,
     'L0_ffn_up_b': 6.39,
     'L0_ffn_down_a': 6.467,
     'L0_ffn_down_b': 6.548}
    for name, (base, spread) in spreads.items():
        noise = np.random.default_rng([zlib.crc32(name.encode()), seed]).standard_normal(out[name].shape)
        drawn = base * np.exp(spread * noise) if base else spread * noise
        out[name] = jnp.asarray(drawn.astype(out[name].dtype))
    for name, factor in factors.items():
        out[name] = (out[name] * factor).astype(out[name].dtype)
    return out
```

```python
from contextlib import ExitStack

import concourse.bass as bass
from concourse import mybir

ALU = mybir.AluOpType
ACT = mybir.ActivationFunctionType
F32 = mybir.dt.float32
F32R = mybir.dt.float32r
BF16 = mybir.dt.bfloat16
AX_X = mybir.AxisListType.X

P = 128
BATCH, SEQ, D = 2, 1024, 512
HEADS, KV_HEADS = 32, 8
HD = D // HEADS
KVD = HD * KV_HEADS
FH = 1376
RANK = 16
EPS = 1e-5
SCALE = HD ** -0.5

DT = D // P
CHUNK = 512
CHUNKS = BATCH * SEQ // CHUNK
CT = CHUNK // P
HT = -(-FH // P)
GU = DT * FH
WCOLS = 2 * GU + HT * D

PAIRS = BATCH * HEADS // 2
KT = SEQ // P
STEPS = PAIRS * KT
TURN = 4 * KT
TURNS = STEPS // TURN
MAXUNITS = 2 * KT
LEAD = 12
T_STEP = 5
PARTS = 3
Q_PARTS = (0, 0, 1, 0, 1, 2)
K_PARTS = (0, 1, 0, 2, 1, 0)
QROWS = HD * len(Q_PARTS)
KROWS = QROWS + PARTS
SBANK = (4, 5, 6, 4)
PVBANK = 7
PIECE = WCOLS // PAIRS
LORA_A_COLS = 2 * D + HT * P
LORA_B_COLS = 2 * FH + D


EVENTS = PAIRS * (MAXUNITS + 1)


def events_before(i, r):
    units = 2 * (r + LEAD)
    if isinstance(i, int) and i == TURNS - 1:
        units = min(units, TURN * 2)
    return units + max(0, r // KT + 1 + (r % KT > T_STEP))


def build(nc, x, w_q, w_k, w_v, w_o, w_ffn, lora_a, lora_b, qs, ks, os_, x2s, out):
    ctx = ExitStack()
    with ctx:
        def sem(name):
            return ctx.enter_context(nc.semaphore(name))

        base = -(-nc.sbuf_base // 32) * 32
        arena = ctx.enter_context(nc.sbuf_tensor("arena", [P, (nc.sbuf_usable_end - base - 64) // 4], F32))
        del arena
        cursor = [base]

        def region(start):
            cursor[0] = start

        def at(name, shape, dt):
            size = 1
            for n in shape[1:]:
                size *= n
            nbytes = size * (2 if dt == BF16 else 4)
            t = nc.alloc_sbuf_tensor_at(name, shape, dt, offset=cursor[0])
            cursor[0] += -(-nbytes // 32) * 32
            return t

        R1 = base
        region(R1)
        w_lo = at("w_lo", [P, WCOLS], F32R)
        R2 = cursor[0]
        w_hi = at("w_hi", [P, WCOLS], F32R)
        R3 = cursor[0]
        region(R1)
        w_sum = at("w_sum", [P, WCOLS], F32)
        region(R1)
        w_raw = at("w_raw", [P, DT, 2 * D + 2 * KVD], F32)
        la_raw = at("la_raw", [P, LORA_A_COLS], F32)
        lb_raw = at("lb_raw", [P, LORA_B_COLS], F32)
        region(R2)
        xin = at("xin", [P, CT, D], F32)
        z = at("z", [P, CT, D], F32)
        zh = at("zh", [P, DT, CHUNK], F32R)
        zl = at("zl", [P, DT, CHUNK], F32R)
        qp = [at(f"qp{i}", [P, PARTS, CHUNK], BF16) for i in range(2)]
        wp_hi = at("wp_hi", [P, DT, D + 2 * KVD], F32R)
        wp_lo = at("wp_lo", [P, DT, D + 2 * KVD], F32R)
        assert cursor[0] <= R3
        region(R3)
        wo_hi = at("wo_hi", [P, DT, D], F32R)
        wo_lo = at("wo_lo", [P, DT, D], F32R)
        ident = at("ident", [P, P], F32)
        ident_b = at("ident_b", [P, P], BF16)
        stats = at("stats", [P, CT, 6], F32)
        mv = at("mv", [P, CT, 2], F32)
        std = at("std", [P, CT], F32)
        rstd = at("rstd", [P, CT], F32)
        eps = at("eps", [P, 1], F32)
        R4 = cursor[0]
        v_all = at("v_all", [P, BATCH * KV_HEADS * KT * HD], F32)
        RQ = cursor[0]
        qaug = [at(f"qaug{i}", [P, 2, SEQ], BF16) for i in range(4)]
        kaug = [at(f"kaug{i}", [P, SEQ], BF16) for i in range(2)]
        v_cur = [at(f"v_cur{i}", [P, KT, 32], F32) for i in range(2)]
        stage = [at(f"stage{i}", [P, PIECE], F32) for i in range(2)]
        RP = cursor[0]
        probs = [at(f"probs{i}", [P, CHUNK], F32) for i in range(8)]
        o_raw = [at(f"o_raw{i}", [P, CHUNK], F32) for i in range(2)]
        negmax = [at(f"negmax{i}", [P, MAXUNITS], F32) for i in range(2)]
        mres = at("mres", [P, 2, MAXUNITS], F32)
        ones = at("ones", [P, MAXUNITS], F32)
        mparts = [at(f"mparts{i}", [P, P], BF16) for i in range(2)]
        mturned = [at(f"mturned{i}", [PARTS * MAXUNITS, P], BF16) for i in range(2)]
        region(RP)
        la = at("la", [P, LORA_A_COLS], F32R)
        lb = at("lb", [P, LORA_B_COLS], F32R)
        region(RQ)
        res = [at(f"res{i}", [P, CHUNK], F32) for i in range(2)]
        region(R4)
        oc = at("oc", [P, CHUNK], F32)
        den = at("den", [P, CHUNK], F32)
        oh = at("oh", [P, DT, CHUNK], F32R)
        ol = at("ol", [P, DT, CHUNK], F32R)
        xz = at("xz", [P, CT, D], F32)
        z2h = at("z2h", [P, DT, CHUNK], F32R)
        z2l = at("z2l", [P, DT, CHUNK], F32R)
        act = [at(f"act{i}", [P, CHUNK], F32) for i in range(2)]
        hh = [at(f"hh{i}", [P, CHUNK], F32R) for i in range(2)]
        hl = [at(f"hl{i}", [P, CHUNK], F32R) for i in range(2)]
        x2 = [at(f"x2_{i}", [P, D], F32) for i in range(2)]

        psum = ctx.enter_context(nc.psum_tensor("psum", [P, 8 * 512], F32))
        bank = [psum[:, 512 * i:512 * (i + 1)] for i in range(8)]
        maxslot = [psum[:, 0:1024], psum[:, 1024:2048]]

        s_x = [sem(f"x_loaded{j}") for j in range(CT)]
        s_w = sem("proj_weights_loaded")
        s_lora = sem("lora_loaded")
        s_zero = sem("lora_zeroed")
        s_const = sem("constants_set")
        s_ones = sem("ones_set")
        s_whi = sem("proj_weights_hi")
        s_wlo = sem("proj_weights_lo")
        s_wo = sem("wo_split")
        s_la = sem("lora_split")
        s_st = sem("ln_stats")
        s_mv = sem("ln_mean_var")
        s_sd = sem("ln_std")
        s_rs = sem("ln_rstd")
        s_z = sem("ln_normed")
        s_tr = sem("z_turned")
        s_zh = sem("z_hi")
        s_zl = sem("z_lo")
        s_proj = sem("projected")
        s_q1 = sem("part1")
        s_res = sem("part1_rest")
        s_q2 = sem("part2")
        s_q3 = sem("part3")
        s_vev = sem("v_kept")
        s_qst = [sem(f"qk_stored{i}") for i in range(2)]
        s_lp = sem("lora_product")
        s_lev = [sem("lora_kept_act"), sem("lora_kept_dve")]
        s_q = [sem(f"q_loaded{i}") for i in range(4)]
        s_k = [sem(f"k_loaded{i}") for i in range(2)]
        s_v = sem("v_placed")
        s_score = sem("scores")
        s_exp = sem("exps")
        s_pv = sem("pv_steps")
        s_ev = sem("o_kept")
        s_od = [sem(f"o_stored{i}") for i in range(2)]
        s_max = sem("max_scores")
        s_mred = sem("max_reduced")
        s_pp = sem("max_split_steps")
        s_split = sem("max_split")
        s_mrow = [sem(f"max_rows{i}") for i in range(2)]
        s_stage = [sem(f"weights_staged{i}") for i in range(2)]
        s_wadd = sem("weights_added")
        s_wh = sem("weights_hi")
        s_wl = sem("weights_lo")
        s_oc = sem("o_loaded")
        s_rl = sem("den_inverted")
        s_on = sem("o_normed")
        s_oh = sem("o_hi")
        s_ol = sem("o_lo")
        s_xz = sem("x_reloaded")
        s_full = sem("ring_full")
        s_free = sem("ring_free")
        s_add = sem("x2_summed")
        s_x2st = sem("x2_stored")
        s_st2 = sem("ln2_stats")
        s_mv2 = sem("ln2_mean_var")
        s_sd2 = sem("ln2_std")
        s_rs2 = sem("ln2_rstd")
        s_z2 = sem("ln2_normed")
        s_zh2 = sem("z2_hi")
        s_zl2 = sem("z2_lo")
        s_silu = sem("silu")
        s_hh = sem("hidden_hi")
        s_hl = sem("hidden_lo")
        s_down = sem("down_steps")
        s_accr = sem("acc_ready")
        s_acc = sem("acc_taken")
        s_x2l = [sem(f"x2_loaded{i}") for i in range(2)]
        s_out = [sem(f"out_stored{i}") for i in range(2)]

        lora_tiles = []
        for which in range(2):
            for d in range(DT):
                for c0 in range(0, FH, 512):
                    n = min(512, FH - c0)
                    lora_tiles.append((which * D + d * P, which * FH + c0, n, which * GU + d * FH + c0))
        for h in range(HT):
            lora_tiles.append((2 * D + h * P, 2 * FH, D, 2 * GU + h * D))

        def gate_w(w, d, h, n):
            return w[:, d * FH + h * P:d * FH + h * P + n]

        def up_w(w, d, h, n):
            return w[:, GU + d * FH + h * P:GU + d * FH + h * P + n]

        def down_w(w, h, n):
            return w[0:n, 2 * GU + h * D:2 * GU + (h + 1) * D]

        def rows_of(h):
            return min(P, FH - h * P)

        USES = [("G", h, h % 2) for h in range(8)] + [("O", 0, 0), ("O", 1, 1)] \
            + [("G", 8, 0), ("G", 9, 1), ("G", 10, 0), ("T", 0, 1), ("T", 1, 0)]
        LAST_USES = [u for u in USES if u[0] == "G"]
        FIRST_USES = [("O", 0, 0), ("O", 1, 1), ("T", 0, 1), ("T", 1, 0)]
        PER = len(USES)
        AHEAD = len(FIRST_USES)

        def use_index(c, k):
            return AHEAD + PER * c + k

        def slot(i, part):
            return bank[4 + 2 * i + part]

        block = ctx.enter_context(nc.Block())

        def hidden_read(engine, c, h):
            if h == 0:
                if not isinstance(c, int) or c > 0:
                    engine.wait_ge(s_accr, CT * c)
            elif h > 1:
                engine.wait_ge(s_down, (HT - 1) * c + h - 1)

        @block.sync
        def _(sp):
            def load_x(c, j):
                if c:
                    sp.wait_ge(s_z, CT * (c - 1) + j + 1)
                t = CT * c + j
                sp.dma_start(xin[:, j, :], x[t * P:(t + 1) * P, :]).then_inc(s_x[j], 16)

            for j in range(CT):
                load_x(0, j)
            sp.dma_start(w_raw[:, :, 0:D], w_q.rearrange("(t p) n -> p t n", p=P)).then_inc(s_w, 16)
            sp.dma_start(w_raw[:, :, D:D + KVD], w_k.rearrange("(t p) n -> p t n", p=P)).then_inc(s_w, 16)
            sp.dma_start(w_raw[:, :, D + KVD:D + 2 * KVD],
                         w_v.rearrange("(t p) n -> p t n", p=P)).then_inc(s_w, 16)
            sp.dma_start(w_raw[:, :, D + 2 * KVD:2 * D + 2 * KVD],
                         w_o.rearrange("(t p) n -> p t n", p=P)).then_inc(s_w, 16)
            sp.wait_ge(s_zero, 2)
            for quad in range(4):
                sp.dma_start(la_raw[32 * quad:32 * quad + RANK, :], lora_a).then_inc(s_lora, 16)
                sp.dma_start(lb_raw[32 * quad:32 * quad + RANK, :], lora_b).then_inc(s_lora, 16)

            for c in range(CHUNKS):
                if c + 1 < CHUNKS:
                    for j in range(CT):
                        load_x(c + 1, j)
                b, h = c // 2, c % 2
                for m in range(5):
                    sp.wait_ge(s_q3, 5 * c + m + 1)
                    dst = (qs[:, b * D + m * P:b * D + (m + 1) * P, h * CHUNK:(h + 1) * CHUNK] if m < 4
                           else ks[:, b * KVD:(b + 1) * KVD, h * CHUNK:(h + 1) * CHUNK])
                    sp.dma_start(dst.rearrange("t p n -> p t n"), qp[m % 2][:, :, :]).then_inc(s_qst[m % 2], 16)

            def load_q(i, r):
                row = (4 * i + r) * 2 * HD
                for s, part in enumerate(Q_PARTS):
                    sp.dma_start(qaug[r % 4][HD * s:HD * (s + 1), :, :],
                                 qs[part, bass.ds(row, 2 * HD), :].rearrange("(h d) n -> d h n", d=HD))\
                      .then_inc(s_q[r % 4], 16)

            def load_k(i, r):
                row = (2 * i + r) * HD
                for s, part in enumerate(K_PARTS):
                    sp.dma_start(kaug[r % 2][HD * s:HD * (s + 1), :], ks[part, bass.ds(row, HD), :])\
                      .then_inc(s_k[r % 2], 16)

            def load_piece(i, r):
                sp.dma_start(stage[r % 2][:, :], w_ffn[:, bass.ds((4 * i + r) * PIECE, PIECE)])\
                  .then_inc(s_stage[r % 2], 16)

            def place_max(i, r):
                last = isinstance(i, int) and 4 * i + r == PAIRS - 1
                sp.wait_ge(s_mred, EVENTS if last else 68 * i + 17 * r + 21)
                for part in range(PARTS):
                    sp.dma_start(qaug[r % 4][QROWS + part:QROWS + part + 1, :, :],
                                 mturned[r % 2][MAXUNITS * part:MAXUNITS * (part + 1), :])\
                      .then_inc(s_mrow[r % 2], 16)

            def store_o(i, r):
                sp.wait_ge(s_ev, 4 * i + r + 1)
                sp.dma_start(os_[bass.ds((4 * i + r) * P, P), :], o_raw[r % 2][:, :]).then_inc(s_od[r % 2], 16)

            sp.wait_ge(s_qst[0], 16 * 3 * CHUNKS)
            sp.wait_ge(s_qst[1], 16 * 2 * CHUNKS)
            for r in range(2):
                load_k(0, r)
            for r in range(4):
                load_q(0, r)
            for r in range(2):
                load_piece(0, r)
            place_max(0, 0)

            def turn(i, last):
                for r in range(4):
                    if not (last and r == 3):
                        place_max(i, r + 1)
                    if not (last and r >= 2):
                        sp.wait_ge(s_wadd, 4 * i + r + 1)
                        load_piece(i, r + 2)
                    if not last:
                        sp.wait_ge(s_score, 4 * KT * (4 * i + r + 1))
                        load_q(i, r + 4)
                        if r % 2:
                            load_k(i, r // 2 + 2)
                    store_o(i, r)

            with sp.Fori(0, TURNS - 1) as i:
                turn(i, False)
            turn(TURNS - 1, True)

            for i in range(2):
                sp.wait_ge(s_od[i], 16 * PAIRS // 2)
            sp.wait_ge(s_pv, STEPS)
            sp.wait_ge(s_wadd, PAIRS)

            o_rows = os_.rearrange("(g h r) n -> g h r n", h=2, r=32)

            def load_o(c):
                b, h = c // 2, c % 2
                for kk in range(DT):
                    if 4 * c + kk:
                        sp.wait_ge(s_ol, 4 * c + kk)
                    g = b * HEADS + kk * 8
                    sp.dma_start(oc[:, :], o_rows[g:g + 8, h, 0:HD, :]).then_inc(s_oc, 16)
                    sp.dma_start(den[:, :], o_rows[g:g + 8, h, HD:HD + 1, :].broadcast_to((8, HD, CHUNK)))\
                      .then_inc(s_oc, 16)

            def load_xz(c):
                if c:
                    sp.wait_ge(s_full, use_index(c - 1, 0))
                sp.dma_start(xz[:, :, :], x[c * CHUNK:(c + 1) * CHUNK, :].rearrange("(j p) n -> p j n", p=P))\
                  .then_inc(s_xz, 16)

            def store_x2(c):
                sp.wait_ge(s_free, 2 if c == 0 else use_index(c - 1, 9) + 1)
                sp.dma_start(x2s[c], xz[:, :, :].rearrange("p j n -> p (j n)")).then_inc(s_x2st, 16)

            def load_x2(c, j):
                if 4 * c + j >= 2:
                    sp.wait_ge(s_out[j % 2], 16 * ((4 * c + j) // 2))
                sp.dma_start(x2[j % 2][:, :], x2s[c, :, j * D:(j + 1) * D]).then_inc(s_x2l[j % 2], 16)

            load_xz(0)
            load_o(0)
            store_x2(0)
            for c in range(CHUNKS):
                if c == 0:
                    sp.wait_ge(s_x2st, 16)
                load_x2(c, 0)
                load_x2(c, 1)
                if c + 1 < CHUNKS:
                    load_xz(c + 1)
                    load_o(c + 1)
                    store_x2(c + 1)
                for j in range(CT):
                    sp.wait_ge(s_acc, CT * c + j + 1)
                    t = CT * c + j
                    sp.dma_start(out[t * P:(t + 1) * P, :], x2[j % 2][:, :]).then_inc(s_out[j % 2], 16)
                    if j < 2:
                        load_x2(c, j + 2)
            for i in range(2):
                sp.wait_ge(s_out[i], 16 * 2 * CHUNKS)

        @block.gpsimd
        def _(pool):
            pool.memset(la_raw[:, :], 0.0).then_inc(s_zero, 1)
            pool.memset(lb_raw[:, :], 0.0).then_inc(s_zero, 1)
            pool.memset(ident[:, :], 0.0).then_inc(s_const, 1)
            pool.memset(ident_b[:, :], 0.0).then_inc(s_const, 1)
            pool.memset(eps[:, :], EPS).then_inc(s_const, 1)
            pool.wait_ge(s_const, 3)
            for t in (ident, ident_b):
                pool.affine_select(out=t[:, :], in_=t[:, :], compare_op=ALU.not_equal, fill=1.0, base=0,
                                   pattern=[[-1, P]], channel_multiplier=1).then_inc(s_const, 1)
            pool.wait_ge(s_w, 64)
            wo_raw = w_raw[:, :, D + 2 * KVD:2 * D + 2 * KVD]
            pool.tensor_scalar(wo_hi[:, :, :], wo_raw, 1.0, None, ALU.mult).then_inc(s_wo, 1)
            pool.wait_ge(s_wo, 1)
            pool.tensor_tensor(wo_lo[:, :, :], wo_raw, wo_hi[:, :, :], ALU.subtract).then_inc(s_wo, 1)
            def split_max(i, r):
                par = r % 2
                n = 4 * i + r
                step = 4 * n
                parts = [mparts[par][:, MAXUNITS * k:MAXUNITS * (k + 1)] for k in range(PARTS)]
                if not isinstance(i, int) or n > 0:
                    pool.wait_ge(s_wadd, n)
                if not isinstance(i, int) or n > 1:
                    pool.wait_ge(s_wh, n - 1)
                    pool.wait_ge(s_max, 68 * i + 17 * (r - 2) + 21)
                pool.wait_ge(s_mred, 68 * i + 17 * r + 16)
                pool.tensor_tensor(parts[0], negmax[par][:, :], ones[:, :], ALU.mult).then_inc(s_pp, 1)
                pool.wait_ge(s_pp, step + 1)
                pool.tensor_tensor(mres[:, 0, :], negmax[par][:, :], parts[0], ALU.subtract).then_inc(s_pp, 1)
                pool.wait_ge(s_pp, step + 2)
                pool.tensor_tensor(parts[1], mres[:, 0, :], ones[:, :], ALU.mult).then_inc(s_pp, 1)
                pool.wait_ge(s_pp, step + 3)
                pool.tensor_tensor(mres[:, 1, :], mres[:, 0, :], parts[1], ALU.subtract).then_inc(s_pp, 1)
                pool.wait_ge(s_pp, step + 4)
                pool.tensor_tensor(parts[2], mres[:, 1, :], ones[:, :], ALU.mult).then_inc(s_split, 1)

            def place_v(i, r):
                if not isinstance(i, int) or i > 0 or r >= 2:
                    pool.wait_ge(s_pv, 2 * KT * (2 * i + r - 1))
                pool.tensor_copy(v_cur[r % 2][:, :, 0:HD],
                                 v_all[:, bass.ds((2 * i + r) * KT * HD, KT * HD)]
                                 .rearrange("p (k d) -> p k d", d=HD)).then_inc(s_v, 1)

            def add_lora(n, par, staged):
                cols = bass.ds(n * PIECE, PIECE)
                pool.wait_ge(s_stage[par], staged)
                pool.tensor_tensor(w_sum[:, cols], w_sum[:, cols], stage[par][:, :], ALU.add)\
                    .then_inc(s_wadd, 1)

            def high_weights(n):
                cols = bass.ds(n * PIECE, PIECE)
                pool.tensor_copy(w_hi[:, cols], w_sum[:, cols]).then_inc(s_wh, 1)

            def low_weights(n):
                cols = bass.ds(n * PIECE, PIECE)
                pool.tensor_tensor(w_lo[:, cols], w_sum[:, cols], w_hi[:, cols], ALU.subtract)\
                    .then_inc(s_wl, 1)

            def prepare_pieces(i, r):
                n = 4 * i + r
                add_lora(n, r % 2, 16 * (2 * i + r // 2 + 1))
                if not isinstance(i, int) or n >= 1:
                    high_weights(n - 1)
                if not isinstance(i, int) or n >= 2:
                    low_weights(n - 2)

            pool.wait_ge(s_ones, 7)
            pool.wait_ge(s_vev, CHUNKS)
            pool.wait_ge(s_lev[0], (len(lora_tiles) + 1) // 2)
            pool.wait_ge(s_lev[1], len(lora_tiles) // 2)

            def turn(i):
                for r in range(4):
                    split_max(i, r)
                    if r % 2 == 0:
                        place_v(i, r // 2)
                    prepare_pieces(i, r)

            turn(0)
            with pool.Fori(1, TURNS) as i:
                turn(i)
            pool.wait_ge(s_wadd, PAIRS)
            high_weights(PAIRS - 1)
            pool.wait_ge(s_wh, PAIRS - 1)
            low_weights(PAIRS - 2)
            pool.wait_ge(s_wh, PAIRS)
            low_weights(PAIRS - 1)

            def norm_o(c):
                for kk in range(DT):
                    n = DT * c + kk
                    pool.wait_ge(s_rl, n + 1)
                    pool.tensor_tensor(oc[:, :], oc[:, :], den[:, :], ALU.mult).then_inc(s_on, 1)
                    pool.wait_ge(s_oh, n + 1)
                    pool.tensor_tensor(ol[:, kk, :], oc[:, :], oh[:, kk, :], ALU.subtract).then_inc(s_ol, 1)

            with pool.Fori(0, CHUNKS) as c:
                norm_o(c)

        @block.scalar
        def _(a):
            def std_of(c, stds, count):
                a.wait_ge(count, CT * (c + 1))
                a.activation(std[:, :], mv[:, :, 1], ACT.Sqrt, bias=eps[:, 0:1]).then_inc(stds, 1)

            a.wait_ge(s_w, 64)
            a.activation(wp_hi[:, :, :], w_raw[:, :, 0:D + 2 * KVD], ACT.Copy).then_inc(s_whi, 1)
            a.wait_ge(s_const, 3)
            std_of(0, s_sd, s_mv)

            for c in range(CHUNKS):
                for d in range(DT):
                    a.wait_ge(s_tr, DT * c + d + 1)
                    if c and d == 0:
                        a.wait_ge(s_proj, 6 * c)
                    a.activation(zh[:, d, :], bank[d], ACT.Copy).then_inc(s_zh, 1)
                if c + 1 < CHUNKS:
                    std_of(c + 1, s_sd, s_mv)
                for m in range(5):
                    n = 5 * c + m
                    a.wait_ge(s_proj, 6 * c + m + 1)
                    if n >= 2:
                        done = 3 * c + m // 2 if m % 2 == 0 else 2 * c + m // 2
                        if done:
                            a.wait_ge(s_qst[m % 2], 16 * done)
                    a.activation(qp[m % 2][:, 0, :], bank[(4, 5, 6, 7, 4)[m]], ACT.Copy).then_inc(s_q1, 1)
                    a.wait_ge(s_res, n + 1)
                    a.activation(qp[m % 2][:, 1, :], res[n % 2][:, :], ACT.Copy).then_inc(s_q2, 1)
                a.wait_ge(s_proj, 6 * c + 6)
                b, h = c // 2, c % 2
                kept = v_all[:, :].rearrange("p (b k t d) -> p b k t d", b=BATCH, k=KV_HEADS, t=KT)
                a.activation(kept[:, b, :, CT * h:CT * (h + 1), :],
                             bank[5].rearrange("p (t k d) -> p k t d", t=CT, k=KV_HEADS), ACT.Copy)\
                    .then_inc(s_vev, 1)

            a.wait_ge(s_wo, 2)
            a.wait_ge(s_wlo, 1)
            a.wait_ge(s_la, 5)
            for n in range(0, len(lora_tiles), 2):
                _, _, cols, at0 = lora_tiles[n]
                a.wait_ge(s_lp, n + 1)
                a.activation(w_sum[:, at0:at0 + cols], bank[n % 8][:, 0:cols], ACT.Copy).then_inc(s_lev[0], 1)

            def exp_tile(i, r, s):
                t = TURN * i + r
                a.wait_ge(s_score, 4 * t + s + 1)
                if s == 0 and r >= 2:
                    a.wait_ge(s_pv, t - 1)
                a.activation(probs[(r % 2) * 4 + s][:, :], bank[SBANK[s]], ACT.Exp, scale=SCALE)\
                    .then_inc(s_exp, 1)

            def keep_o(i, r):
                a.wait_ge(s_pv, KT * (4 * i + r + 1))
                if not isinstance(i, int) or 2 * i + r // 2 > 0:
                    a.wait_ge(s_od[r % 2], 16 * (2 * i + r // 2))
                a.activation(o_raw[r % 2][:, :], bank[PVBANK], ACT.Copy).then_inc(s_ev, 1)

            def step(i, r):
                for s in range(4):
                    exp_tile(i, r, s)
                    if s == 1 and r % KT == 1 and r >= KT:
                        keep_o(i, r // KT - 1)

            for r in range(TURN + 2):
                step(0, r)
            with a.Fori(1, TURNS - 1) as i:
                for r in range(2, TURN + 2):
                    step(i, r)
            for r in range(2, TURN):
                step(TURNS - 1, r)
            keep_o(TURNS - 1, 3)

            def high_o(c, kk):
                n = DT * c + kk
                a.wait_ge(s_on, n + 1)
                a.activation(oh[:, kk, :], oc[:, :], ACT.Copy).then_inc(s_oh, 1)

            def turned(c, part, k):
                a.wait_ge(s_full, k + 1)
                for q in range(2):
                    a.activation(z2h[:, 2 * part + q, :], slot((1, 0)[part], q), ACT.Copy).then_inc(s_zh2, 1)

            def gate(c, h, k, i):
                n = HT * c + h
                rows = rows_of(h)
                a.wait_ge(s_full, k + 1)
                if not (isinstance(c, int) and c == 0 and h < 2):
                    a.wait_ge(s_hl, n if h == 0 else n - 1)
                a.activation(act[h % 2][0:rows, :], slot(i, 0)[0:rows, :], ACT.Silu).then_inc(s_silu, 1)
                a.wait_ge(s_free, k + 1)
                hidden_read(a, c, h)
                a.activation(hh[h % 2][0:rows, :], act[h % 2][0:rows, :], ACT.Copy).then_inc(s_hh, 1)

            for kk in range(DT):
                high_o(0, kk)
            std_of(0, s_sd2, s_mv2)
            turned(0, 0, 2)
            turned(0, 1, 3)

            def chunk(c, last):
                k = 0
                for what, n, i in (LAST_USES if last else USES):
                    at_k = use_index(c, k)
                    if what == "G":
                        gate(c, n, at_k, i)
                        if not last and 1 <= n <= DT:
                            high_o(c + 1, n - 1)
                        if not last and n == 9:
                            std_of(c + 1, s_sd2, s_mv2)
                    if what == "T":
                        turned(c + 1, n, at_k)
                    k += 1

            chunk(0, False)
            with a.Fori(1, CHUNKS - 1) as c:
                chunk(c, False)
            chunk(CHUNKS - 1, True)

        @block.vector
        def _(v):
            def stats_of(j, src, loaded, count, stat):
                v.wait_ge(loaded, count)
                v.bn_stats(stats[:, j, :], src[:, j, :]).then_inc(stat, 1)

            def rstd_of(c, stds, rstds):
                v.wait_ge(stds, c + 1)
                v.reciprocal(rstd[:, :], std[:, :]).then_inc(rstds, 1)
                v.wait_ge(rstds, c + 1)

            def norm(c):
                for j in range(CT):
                    stats_of(j, xin, s_x[j], 16 * (c + 1), s_st)
                v.wait_ge(s_st, CT * (c + 1))
                for j in range(CT):
                    v.bn_aggr(mv[:, j, :], stats[:, j, :]).then_inc(s_mv, 1)
                rstd_of(c, s_sd, s_rs)
                if c:
                    v.wait_ge(s_tr, DT * c)
                for j in range(CT):
                    v.tensor_scalar(z[:, j, :], xin[:, j, :], mv[:, j, 0:1], rstd[:, j:j + 1],
                                    ALU.subtract, ALU.mult).then_inc(s_z, 1)

            for i in range(2):
                v.memset(kaug[i][QROWS:KROWS, :], 1.0).then_inc(s_ones, 1)
                v.memset(v_cur[i][:, :, :], 1.0).then_inc(s_ones, 1)
            norm(0)
            v.wait_ge(s_whi, 1)
            v.tensor_tensor(wp_lo[:, :, :], w_raw[:, :, 0:D + 2 * KVD], wp_hi[:, :, :], ALU.subtract)\
                .then_inc(s_wlo, 1)

            for c in range(CHUNKS):
                for d in range(DT):
                    v.wait_ge(s_zh, DT * c + d + 1)
                    v.tensor_tensor(zl[:, d, :], bank[d], zh[:, d, :], ALU.subtract).then_inc(s_zl, 1)
                if c == 0:
                    v.wait_ge(s_lora, 16 * 8)
                    v.tensor_copy(la[:, :], la_raw[:, :]).then_inc(s_la, 1)
                    v.tensor_copy(lb[:, :], lb_raw[:, :]).then_inc(s_la, 1)
                    v.wait_ge(s_la, 2)
                    for t, raw, q0, q1 in ((la, la_raw, 2, 4), (lb, lb_raw, 1, 2), (lb, lb_raw, 3, 4)):
                        rows = slice(32 * q0, 32 * q1)
                        v.tensor_tensor(t[rows, :], raw[rows, :], t[rows, :], ALU.subtract).then_inc(s_la, 1)
                if c + 1 < CHUNKS:
                    norm(c + 1)
                for m in range(5):
                    n = 5 * c + m
                    v.wait_ge(s_q1, n + 1)
                    if n >= 2:
                        v.wait_ge(s_q2, n - 1)
                        v.wait_ge(s_q3, n - 1)
                    v.tensor_tensor(res[n % 2][:, :], bank[(4, 5, 6, 7, 4)[m]], qp[m % 2][:, 0, :], ALU.subtract)\
                        .then_inc(s_res, 1)
                    v.wait_ge(s_q2, n + 1)
                    v.tensor_tensor(qp[m % 2][:, 2, :], res[n % 2][:, :], qp[m % 2][:, 1, :], ALU.subtract)\
                        .then_inc(s_q3, 1)

            v.wait_ge(s_wo, 2)
            for n in range(1, len(lora_tiles), 2):
                _, _, cols, at0 = lora_tiles[n]
                v.wait_ge(s_lp, n + 1)
                v.tensor_copy(w_sum[:, at0:at0 + cols], bank[n % 8][:, 0:cols]).then_inc(s_lev[1], 1)

            v.wait_ge(s_lp, len(lora_tiles))
            for i in range(2):
                v.memset(mparts[i][:, :], 0.0).then_inc(s_ones, 1)
            v.memset(ones[:, :], 1.0).then_inc(s_ones, 1)

            def max_step(i, r, units, turned):
                e = events_before(i, r)
                for q in range(units):
                    u = 2 * (r + LEAD) + q
                    pair, unit = u // MAXUNITS, u % MAXUNITS
                    if unit == 0 and (pair >= 2 or not isinstance(i, int) or i > 0):
                        v.wait_ge(s_split, 4 * i + pair - 1)
                    v.wait_ge(s_max, 68 * i + e + q + 1)
                    v.tensor_reduce(negmax[pair % 2][:, unit:unit + 1], maxslot[(e + q) % 2], AX_X, ALU.max,
                                    negate=True).then_inc(s_mred, 1)
                if turned:
                    e += units
                    pair = r // KT + 1
                    v.wait_ge(s_max, 68 * i + e + 1)
                    if not isinstance(i, int) or 2 * i + pair // 2 > 0:
                        v.wait_ge(s_mrow[pair % 2], 16 * PARTS * (2 * i + pair // 2))
                    v.tensor_copy(mturned[pair % 2][:, :],
                                  maxslot[e % 2][0:PARTS * MAXUNITS, 0:P // 2].bitcast(BF16))\
                        .then_inc(s_mred, 1)

            def units_in(i, r):
                return 2 if i < TURNS - 1 or r < TURN - LEAD else 0

            for r in range(-LEAD, TURN):
                max_step(0, r, 2, r % KT == T_STEP and r > -KT)
            with v.Fori(1, TURNS - 1) as i:
                for r in range(TURN):
                    max_step(i, r, 2, r % KT == T_STEP)
            for r in range(TURN):
                max_step(TURNS - 1, r, units_in(TURNS - 1, r), r % KT == T_STEP and r < TURN - KT)

            def invert(c, kk):
                n = DT * c + kk
                v.wait_ge(s_oc, 32 * (n + 1))
                v.reciprocal(den[:, :], den[:, :]).then_inc(s_rl, 1)

            def add_x(c, part, k, i):
                v.wait_ge(s_full, k + 1)
                if part == 0:
                    v.wait_ge(s_xz, 16 * (c + 1))
                else:
                    v.wait_ge(s_st2, CT * c + 2)
                for q in range(2):
                    j = 2 * part + q
                    v.tensor_tensor(xz[:, j, :], slot(i, q), xz[:, j, :], ALU.add)\
                        .then_inc((s_add, s_free)[q], 1)
                if part == 1:
                    mean_of(0)
                stats_of(2 * part, xz, s_add, 2 * c + part + 1, s_st2)
                stats_of(2 * part + 1, xz, s_free, k + 1, s_st2)

            def mean_of(part):
                for j in (2 * part, 2 * part + 1):
                    v.bn_aggr(mv[:, j, :], stats[:, j, :]).then_inc(s_mv2, 1)

            def norm2(c):
                rstd_of(c, s_sd2, s_rs2)
                v.wait_ge(s_x2st, 16 * (c + 1))
                for j in range(CT):
                    v.tensor_scalar(xz[:, j, :], xz[:, j, :], mv[:, j, 0:1], rstd[:, j:j + 1],
                                    ALU.subtract, ALU.mult).then_inc(s_z2, 1)

            def low_turned(c, part, k):
                for q in range(2):
                    v.wait_ge(s_zh2, DT * c + 2 * part + q + 1)
                    v.tensor_tensor(z2l[:, 2 * part + q, :], slot((1, 0)[part], q), z2h[:, 2 * part + q, :],
                                    ALU.subtract).then_inc((s_zl2, s_free)[q], 1)

            def hidden(c, h, k, i, means):
                n = HT * c + h
                rows = rows_of(h)
                if means:
                    v.wait_ge(s_st2, CT * (c + 2))
                v.wait_ge(s_silu, n + 1)
                v.tensor_tensor(act[h % 2][0:rows, :], slot(i, 1)[0:rows, :], act[h % 2][0:rows, :],
                                ALU.mult).then_inc(s_free, 1)
                if means:
                    mean_of(1)
                v.wait_ge(s_hh, n + 1)
                hidden_read(v, c, h)
                v.tensor_tensor(hl[h % 2][0:rows, :], act[h % 2][0:rows, :], hh[h % 2][0:rows, :],
                                ALU.subtract).then_inc(s_hl, 1)

            def add_out(c):
                for j in range(CT):
                    v.wait_ge(s_accr, CT * c + j + 1)
                    v.wait_ge(s_x2l[j % 2], 16 * (2 * c + j // 2 + 1))
                    v.tensor_tensor(x2[j % 2][:, :], bank[j], x2[j % 2][:, :], ALU.add).then_inc(s_acc, 1)

            for kk in range(DT):
                invert(0, kk)
            add_x(0, 0, 0, 0)
            add_x(0, 1, 1, 1)
            v.wait_ge(s_st2, CT)
            mean_of(1)
            norm2(0)
            low_turned(0, 0, 2)
            low_turned(0, 1, 3)

            def chunk(c, last):
                k = 0
                for what, n, i in (LAST_USES if last else USES):
                    at_k = use_index(c, k)
                    if what == "G":
                        hidden(c, n, at_k, i, not last and n == 8)
                        if not last and 1 <= n <= DT:
                            invert(c + 1, n - 1)
                        if not last and n == 9:
                            norm2(c + 1)
                        if n == HT - 1:
                            add_out(c)
                    if what == "O":
                        add_x(c + 1, n, at_k, i)
                    if what == "T":
                        low_turned(c + 1, n, at_k)
                    k += 1

            chunk(0, False)
            with v.Fori(1, CHUNKS - 1) as c:
                chunk(c, False)
            chunk(CHUNKS - 1, True)

        @block.tensor
        def _(pe):
            def product(dst, lhs, rhs, first, last):
                n = len(lhs)
                for t, ((lh, ll), (rh, rl)) in enumerate(zip(lhs, rhs)):
                    pe.matmul(dst, lh, rh, start=first and t == 0, stop=False)
                    pe.matmul(dst, ll, rh, start=False, stop=False)
                    ins = pe.matmul(dst, lh, rl, start=False, stop=last and t == n - 1)
                return ins

            def turn_rows(c):
                if not isinstance(c, int) or c > 0:
                    pe.wait_ge(s_zl, DT * c)
                for j in range(CT):
                    pe.wait_ge(s_z, CT * c + j + 1)
                    for d in range(DT):
                        ins = pe.transpose(bank[d][:, j * P:(j + 1) * P], z[:, j, d * P:(d + 1) * P],
                                           ident[:, :])
                        if j == CT - 1:
                            ins.then_inc(s_tr, 1)

            def project(c):
                first = isinstance(c, int) and c == 0
                pe.wait_ge(s_zl, DT * (c + 1))
                for m in range(5):
                    if m == 0 and not first:
                        pe.wait_ge(s_res, 5 * c)
                    if m == 1 and not first:
                        pe.wait_ge(s_vev, c)
                    if m in (2, 3) and not first:
                        pe.wait_ge(s_res, 5 * c - 4 + m)
                    if m == 4:
                        pe.wait_ge(s_res, 5 * c + 1)
                    w = slice(m * P, (m + 1) * P)
                    product(bank[(4, 5, 6, 7, 4)[m]],
                            [(wp_hi[:, d, w], wp_lo[:, d, w]) for d in range(DT)],
                            [(zh[:, d, :], zl[:, d, :]) for d in range(DT)], True, True).then_inc(s_proj, 1)
                pe.wait_ge(s_res, 5 * c + 2)
                w = slice(D + KVD, D + 2 * KVD)
                for j in range(CT):
                    rows = slice(j * P, (j + 1) * P)
                    ins = product(bank[5][:, rows],
                                  [(zh[:, d, rows], zl[:, d, rows]) for d in range(DT)],
                                  [(wp_hi[:, d, w], wp_lo[:, d, w]) for d in range(DT)], True, True)
                ins.then_inc(s_proj, 1)

            pe.wait_ge(s_const, 5)
            turn_rows(0)
            pe.wait_ge(s_wlo, 1)
            project(0)
            with pe.Fori(1, CHUNKS) as c:
                turn_rows(c)
                project(c)

            pe.wait_ge(s_la, 5)
            pe.wait_ge(s_zl, DT * CHUNKS)
            pe.wait_ge(s_res, 5 * CHUNKS)
            pe.wait_ge(s_vev, CHUNKS)
            for n, (acol, bcol, cols, _) in enumerate(lora_tiles):
                if n >= 8:
                    pe.wait_ge(s_lev[n % 2], (n - 8) // 2 + 1)
                pe.matmul(bank[n % 8][:, 0:cols], la[:, acol:acol + P], lb[:, bcol:bcol + cols],
                          start=True, stop=True).then_inc(s_lp, 1)

            def max_unit(i, r, q, half):
                e = events_before(i, r) + q
                u = 2 * (r + LEAD) + q
                pair, unit = u // MAXUNITS, u % MAXUNITS
                if unit == 0 and half == 0:
                    pe.wait_ge(s_q[pair % 4], 16 * 6 * (i + pair // 4 + 1))
                    if pair % 2 == 0:
                        pe.wait_ge(s_k[pair // 2 % 2], 16 * 6 * (i + pair // 4 + 1))
                if half == 0 and (not isinstance(i, int) or 68 * i + e >= 2):
                    pe.wait_ge(s_mred, 68 * i + e - 1)
                head, qt = unit // KT, unit % KT
                ins = pe.matmul(maxslot[e % 2][:, half * 512:(half + 1) * 512],
                                qaug[pair % 4][0:QROWS, head, qt * P:(qt + 1) * P],
                                kaug[pair // 2 % 2][0:QROWS, half * 512:(half + 1) * 512],
                                start=True, stop=True)
                if half:
                    ins.then_inc(s_max, 1)

            def turn_max(i, r, units):
                e = events_before(i, r) + units
                pair = r // KT + 1
                pe.wait_ge(s_split, 4 * i + pair + 1)
                pe.wait_ge(s_mred, 68 * i + e - 1)
                pe.transpose(maxslot[e % 2][:, 0:P // 2].bitcast(BF16),
                             mparts[pair % 2][:, :], ident_b[:, :]).then_inc(s_max, 1)

            def score(i, r, s):
                t = TURN * i + r
                pair, kt = r // KT, r % KT
                if kt == 0 and s == 0:
                    pe.wait_ge(s_mrow[pair % 2], 16 * PARTS * (2 * i + pair // 2 + 1))
                if s == 3:
                    pe.wait_ge(s_exp, 4 * t + 1)
                elif not isinstance(i, int) or t > 0:
                    pe.wait_ge(s_exp, 4 * t - (0, 2, 1)[s])
                head, half = s // 2, s % 2
                pe.matmul(bank[SBANK[s]], kaug[pair // 2 % 2][0:KROWS, kt * P:(kt + 1) * P],
                          qaug[pair % 4][0:KROWS, head, half * CHUNK:(half + 1) * CHUNK],
                          start=True, stop=True).then_inc(s_score, 1)

            def pv(i, r):
                t = TURN * i + r
                pair, kt = r // KT, r % KT
                pe.wait_ge(s_exp, 4 * t + 4)
                if kt == 0:
                    if not isinstance(i, int) or 4 * i + pair > 0:
                        pe.wait_ge(s_ev, 4 * i + pair)
                    pe.wait_ge(s_v, 2 * i + pair // 2 + 1)
                for s in range(4):
                    ins = pe.matmul(bank[PVBANK][32 * s:32 * s + 32, :], v_cur[pair // 2 % 2][:, kt, :],
                                    probs[(r % 2) * 4 + s][:, :], start=kt == 0, stop=kt == KT - 1,
                                    skip_group_check=True)
                ins.then_inc(s_pv, 1)

            def step(i, r, with_pv=True, units=2, turned=True):
                for s in range(4):
                    score(i, r, s)
                    if units:
                        max_unit(i, r, s // 2, s % 2)
                if with_pv:
                    pv(i, r - 1)
                if r % KT == T_STEP and turned:
                    turn_max(i, r, units)

            pe.wait_ge(s_lev[0], (len(lora_tiles) + 1) // 2)
            pe.wait_ge(s_lev[1], len(lora_tiles) // 2)
            pe.wait_ge(s_ones, 4)
            for r in range(-LEAD, 0):
                for q in range(2):
                    for half in range(2):
                        max_unit(0, r, q, half)
                if r % KT == T_STEP and r > -KT:
                    turn_max(0, r, 2)
            for r in range(TURN + 1):
                step(0, r, with_pv=r > 0)
            with pe.Fori(1, TURNS - 1) as i:
                for r in range(1, TURN + 1):
                    step(i, r)
            for r in range(1, TURN):
                step(TURNS - 1, r, units=2 if r < TURN - LEAD else 0, turned=r < TURN - KT)
            pv(TURNS - 1, TURN - 1)

            def free_wait(c, k):
                pe.wait_ge(s_free, use_index(c, 0) if k == 0 else use_index(c, k) - 1)

            def out_project(c, part, i):
                pe.wait_ge(s_ol, DT * (c + 1))
                for q in range(2):
                    rows = slice((2 * part + q) * P, (2 * part + q + 1) * P)
                    ins = product(slot(i, q), [(oh[:, d, rows], ol[:, d, rows]) for d in range(DT)],
                                  [(wo_hi[:, d, :], wo_lo[:, d, :]) for d in range(DT)], True, True)
                ins.then_inc(s_full, 1)

            def turn_rows2(c, part, i):
                pe.wait_ge(s_z2, CT * (c + 1))
                for q in range(2):
                    for j in range(CT):
                        d = 2 * part + q
                        ins = pe.transpose(slot(i, q)[:, j * P:(j + 1) * P], xz[:, j, d * P:(d + 1) * P],
                                           ident[:, :])
                ins.then_inc(s_full, 1)

            def gate_up(c, h, i):
                n = rows_of(h)
                for q, cols in enumerate((gate_w, up_w)):
                    ins = product(slot(i, q)[0:n, :], [(cols(w_hi, d, h, n), cols(w_lo, d, h, n)) for d in range(DT)],
                                  [(z2h[:, d, :], z2l[:, d, :]) for d in range(DT)], True, True)
                ins.then_inc(s_full, 1)

            def down(c, h):
                n = rows_of(h)
                pe.wait_ge(s_hl, HT * c + h + 1)
                if h == 0 and (not isinstance(c, int) or c > 0):
                    pe.wait_ge(s_acc, CT * c)
                for j in range(CT):
                    rows = slice(j * P, (j + 1) * P)
                    ins = product(bank[j], [(hh[h % 2][0:n, rows], hl[h % 2][0:n, rows])],
                                  [(down_w(w_hi, h, n), down_w(w_lo, h, n))], h == 0, h == HT - 1)
                    if h == HT - 1:
                        ins.then_inc(s_accr, 1)
                    elif j == CT - 1:
                        ins.then_inc(s_down, 1)

            pe.wait_ge(s_exp, 4 * STEPS)
            pe.wait_ge(s_ev, PAIRS)
            pe.wait_ge(s_mred, 68 * TURNS)
            pe.wait_ge(s_wo, 2)
            out_project(0, 0, 0)
            out_project(0, 1, 1)
            pe.wait_ge(s_free, 2)
            turn_rows2(0, 0, 1)
            turn_rows2(0, 1, 0)
            pe.wait_ge(s_wl, PAIRS)

            def chunk(c, last):
                k = 0
                for what, n, i in (LAST_USES if last else USES):
                    free_wait(c, k)
                    if what == "G":
                        gate_up(c, n, i)
                        if n > 0:
                            down(c, n - 1)
                        if n == HT - 1:
                            down(c, n)
                    if what == "O":
                        out_project(c + 1, n, i)
                    if what == "T":
                        turn_rows2(c + 1, n, i)
                    k += 1

            chunk(0, False)
            with pe.Fori(1, CHUNKS - 1) as c:
                chunk(c, False)
            chunk(CHUNKS - 1, True)


def kernel(**inputs):
    import numpy as np
    import concourse.bacc as bacc
    from concourse.bass_utils import run_bass_kernel_spmd

    def tiles(w):
        t = -(-w.shape[0] // P)
        full = np.zeros((t * P, w.shape[1]), w.dtype)
        full[:w.shape[0]] = w
        return full.reshape(t, P, w.shape[1]).transpose(1, 0, 2).reshape(P, t * w.shape[1])

    a = {n.replace("L0_attn_", "").replace("L0_ffn_", ""): np.asarray(v) for n, v in inputs.items()}
    down_a = np.zeros((RANK, HT * P), a["down_a"].dtype)
    down_a[:, :FH] = a["down_a"]
    arrays = {
        "x": a["x"].reshape(BATCH * SEQ, D),
        "w_q": a["w_q"], "w_k": a["w_k"], "w_v": a["w_v"], "w_o": a["w_o"],
        "w_ffn": np.concatenate([tiles(a["gate_w"].T), tiles(a["up_w"].T), tiles(a["down_w"].T)], axis=1),
        "lora_a": np.concatenate([a["gate_a"], a["up_a"], down_a], axis=1),
        "lora_b": np.concatenate([a["gate_b"].T, a["up_b"].T, a["down_b"].T], axis=1),
    }
    arrays = {n: np.ascontiguousarray(v) for n, v in arrays.items()}
    nc = bacc.Bacc("TRN2", target_bir_lowering=False, num_devices=1)
    args = [nc.dram_tensor(n, v.shape, mybir.dt.from_np(v.dtype), kind="ExternalInput").ap()
            for n, v in arrays.items()]
    args += [
        nc.dram_tensor("q_parts", (PARTS, BATCH * D, SEQ), BF16).ap(),
        nc.dram_tensor("k_parts", (PARTS, BATCH * KVD, SEQ), BF16).ap(),
        nc.dram_tensor("o_sums", (PAIRS * P, CHUNK), F32).ap(),
        nc.dram_tensor("x_plus_attention", (CHUNKS, P, CT * D), F32).ap(),
        nc.dram_tensor("out", (BATCH * SEQ, D), F32, kind="ExternalOutput").ap(),
    ]
    build(nc, *args)
    r = run_bass_kernel_spmd(nc, [arrays], core_ids=[0])
    return r.results[0]["out"].reshape(BATCH, SEQ, D)
```

```python
from contextlib import ExitStack

import concourse.bass as bass
from concourse import mybir

ALU = mybir.AluOpType
ACT = mybir.ActivationFunctionType
F32 = mybir.dt.float32
F32R = mybir.dt.float32r
BF16 = mybir.dt.bfloat16
AX_X = mybir.AxisListType.X

P = 128
BATCH, SEQ, D = 2, 1024, 512
HEADS, KV_HEADS = 32, 8
HD = D // HEADS
KVD = HD * KV_HEADS
FH = 1376
RANK = 16
EPS = 1e-5
SCALE = HD ** -0.5

DT = D // P
CHUNK = 512
CHUNKS = BATCH * SEQ // CHUNK
CT = CHUNK // P
HT = -(-FH // P)
GU = DT * FH
WCOLS = 2 * GU + HT * D

PAIRS = BATCH * HEADS // 2
KT = SEQ // P
STEPS = PAIRS * KT
TURN = 4 * KT
TURNS = STEPS // TURN
MAXUNITS = 2 * KT
TURN_BEHIND = 2
LEAD = 12
INVERT_STEP = 20
O_STEPS = (24, 26)
STD_STEP = 30
T_STEP = 5
PARTS = 3
Q_PARTS = (0, 0, 1, 0, 1, 2)
K_PARTS = (0, 1, 0, 2, 1, 0)
QROWS = HD * len(Q_PARTS)
KROWS = QROWS + PARTS
SBANK = (4, 5, 6, 4)
PVBANK = 7
PIECE = WCOLS // PAIRS
LORA_A_COLS = 2 * D + HT * P
LORA_B_COLS = 2 * FH + D


EVENTS = PAIRS * (MAXUNITS + 1)


def events_before(i, r):
    units = 2 * (r + LEAD)
    if isinstance(i, int) and i == TURNS - 1:
        units = min(units, TURN * 2)
    return units + max(0, r // KT + 1 + (r % KT > T_STEP))


def build(nc, x, w_q, w_k, w_v, w_o, w_ffn, lora_a, lora_b, qs, ks, os_, rs, x2s, out):
    ctx = ExitStack()
    with ctx:
        def sem(name):
            return ctx.enter_context(nc.semaphore(name))

        base = -(-nc.sbuf_base // 32) * 32
        arena = ctx.enter_context(nc.sbuf_tensor("arena", [P, (nc.sbuf_usable_end - base - 64) // 4], F32))
        del arena
        cursor = [base]

        def region(start):
            cursor[0] = start

        def at(name, shape, dt):
            size = 1
            for n in shape[1:]:
                size *= n
            nbytes = size * (2 if dt == BF16 else 4)
            t = nc.alloc_sbuf_tensor_at(name, shape, dt, offset=cursor[0])
            cursor[0] += -(-nbytes // 32) * 32
            return t

        R1 = base
        region(R1)
        w_lo = at("w_lo", [P, WCOLS], F32R)
        R2 = cursor[0]
        w_hi = at("w_hi", [P, WCOLS], F32R)
        R3 = cursor[0]
        region(R1)
        w_sum = at("w_sum", [P, WCOLS], F32)
        region(R1)
        w_raw = at("w_raw", [P, DT, 2 * D + 2 * KVD], F32)
        la_raw = at("la_raw", [P, LORA_A_COLS], F32)
        lb_raw = at("lb_raw", [P, LORA_B_COLS], F32)
        region(R2)
        xin = at("xin", [P, CT, D], F32)
        z = at("z", [P, CT, D], F32)
        zh = [at("zh0", [P, DT, CHUNK], F32R)]
        zl = [at("zl0", [P, DT, CHUNK], F32R)]
        qp = [at(f"qp{i}", [P, PARTS, CHUNK], BF16) for i in range(2)]
        wp_hi = at("wp_hi", [P, DT, D + 2 * KVD], F32R)
        wp_lo = at("wp_lo", [P, DT, D + 2 * KVD], F32R)
        assert cursor[0] <= R3
        region(R3)
        wo_hi = at("wo_hi", [P, DT, D], F32R)
        wo_lo = at("wo_lo", [P, DT, D], F32R)
        ident = at("ident", [P, P], F32)
        ident_b = at("ident_b", [P, P], BF16)
        stats = at("stats", [P, CT, 6], F32)
        mv = at("mv", [P, CT, 2], F32)
        std = at("std", [P, CT], F32)
        rstd = at("rstd", [P, CT], F32)
        eps = at("eps", [P, 1], F32)
        sums = at("sums", [P, 8 * 2 * CHUNK // P], F32)
        R4 = cursor[0]
        v_all = at("v_all", [P, BATCH * KV_HEADS * KT * HD], F32)
        RQ = cursor[0]
        qaug = [at(f"qaug{i}", [P, 2, SEQ], BF16) for i in range(2)]
        kaug = [at("kaug0", [P, SEQ], BF16)]
        v_cur = [at("v_cur0", [P, KT, 32], F32)]
        stage = [at(f"stage{i}", [P, PIECE], F32) for i in range(2)]
        cursor[0] = R4 + 4 * (2 * DT * CHUNK + CT * D)
        qaug += [at(f"qaug{i}", [P, 2, SEQ], BF16) for i in range(2, 4)]
        kaug += [at("kaug1", [P, SEQ], BF16)]
        v_cur += [at("v_cur1", [P, KT, 32], F32)]
        RP = cursor[0]
        probs = [at(f"probs{i}", [P, CHUNK], F32) for i in range(8)]
        o_raw = [at(f"o_raw{i}", [P, CHUNK], F32) for i in range(2)]
        cursor[0] = max(cursor[0], RP + 4 * (LORA_A_COLS + LORA_B_COLS))
        negmax = [at(f"negmax{i}", [P, MAXUNITS], F32) for i in range(2)]
        mres = at("mres", [P, 2, MAXUNITS], F32)
        ones = at("ones", [P, MAXUNITS], F32)
        mparts = [at(f"mparts{i}", [P, P], BF16) for i in range(2)]
        mturned = [at(f"mturned{i}", [PARTS * MAXUNITS, P], BF16) for i in range(2)]
        region(RP)
        la = at("la", [P, LORA_A_COLS], F32R)
        lb = at("lb", [P, LORA_B_COLS], F32R)
        region(RQ)
        zh += [at("zh1", [P, DT, CHUNK], F32R)]
        cursor[0] += 2 * SEQ + 4 * KT * 32
        zl += [at("zl1", [P, DT, CHUNK], F32R)]
        res = [at(f"res{i}", [P, CHUNK], F32) for i in range(2)]
        assert cursor[0] <= RQ + 4 * (DT * CHUNK + CT * D) + 4 * SEQ * 2
        region(R4)
        den = at("den", [P, DT, CHUNK], F32)
        o_in = at("o_in", [P, DT, CHUNK], F32)
        region(R4)
        oh = at("oh", [P, DT, CHUNK], F32R)
        ol = at("ol", [P, DT, CHUNK], F32R)
        xz = at("xz", [P, CT, D], F32)
        z2h = at("z2h", [P, DT, CHUNK], F32R)
        z2l = at("z2l", [P, DT, CHUNK], F32R)
        act = [at(f"act{i}", [P, CHUNK], F32) for i in range(2)]
        hh = [at(f"hh{i}", [P, CHUNK], F32R) for i in range(2)]
        hl = [at(f"hl{i}", [P, CHUNK], F32R) for i in range(2)]
        x2 = [at(f"x2_{i}", [P, D], F32) for i in range(CT)]

        psum = ctx.enter_context(nc.psum_tensor("psum", [P, 8 * 512], F32))
        bank = [psum[:, 512 * i:512 * (i + 1)] for i in range(8)]
        maxslot = [psum[:, 0:1024], psum[:, 1024:2048]]

        s_x = [sem(f"x_loaded{j}") for j in range(CT)]
        s_w = sem("proj_weights_loaded")
        s_wor = sem("wo_loaded")
        s_lora = sem("lora_loaded")
        s_zero = sem("lora_zeroed")
        s_const = sem("constants_set")
        s_ones = sem("ones_set")
        s_whi = sem("proj_weights_hi")
        s_wlo = sem("proj_weights_lo")
        s_wo = sem("wo_split")
        s_la = sem("lora_split")
        s_st = sem("ln_stats")
        s_mv = sem("ln_mean_var")
        s_sd = sem("ln_std")
        s_rs = sem("ln_rstd")
        s_z = sem("ln_normed")
        s_tr = sem("z_turned")
        s_zh = sem("z_hi")
        s_zl = sem("z_lo")
        s_proj = sem("projected")
        s_q1 = sem("part1")
        s_res = sem("part1_rest")
        s_q2 = sem("part2")
        s_q3 = sem("part3")
        s_vev = sem("v_kept")
        s_qst = [sem(f"qk_stored{i}") for i in range(2)]
        s_lp = sem("lora_product")
        s_lev = [sem("lora_kept_act"), sem("lora_kept_dve")]
        s_q = [sem(f"q_loaded{i}") for i in range(4)]
        s_k = [sem(f"k_loaded{i}") for i in range(2)]
        s_v = sem("v_placed")
        s_score = sem("scores")
        s_exp = sem("exps")
        s_pv = sem("pv_steps")
        s_ev = sem("o_kept")
        s_od = [sem(f"o_stored{i}") for i in range(2)]
        s_max = sem("max_scores")
        s_mred = sem("max_reduced")
        s_pp = sem("max_split_steps")
        s_split = sem("max_split")
        s_mrow = [sem(f"max_rows{i}") for i in range(2)]
        s_stage = [sem(f"weights_staged{i}") for i in range(2)]
        s_wadd = sem("weights_added")
        s_wh = sem("weights_hi")
        s_wl = sem("weights_lo")
        s_sum = sem("sums_loaded")
        s_inv = sem("sums_inverted")
        s_rst = sem("inverted_stored")
        s_oc = [sem(f"o_loaded{i}") for i in range(DT)]
        s_on = sem("o_normed")
        s_oh = sem("o_hi")
        s_ol = sem("o_lo")
        s_xz = sem("x_reloaded")
        s_full = sem("ring_full")
        s_free = sem("ring_free")
        s_add = sem("x2_summed")
        s_x2st = sem("x2_stored")
        s_st2 = sem("ln2_stats")
        s_mv2 = sem("ln2_mean_var")
        s_sd2 = sem("ln2_std")
        s_rs2 = sem("ln2_rstd")
        s_z2 = sem("ln2_normed")
        s_zh2 = sem("z2_hi")
        s_zl2 = sem("z2_lo")
        s_silu = sem("silu")
        s_hh = sem("hidden_hi")
        s_hl = sem("hidden_lo")
        s_down = sem("down_steps")
        s_accr = sem("acc_ready")
        s_acc = sem("acc_taken")
        s_x2l = [sem(f"x2_loaded{i}") for i in range(CT)]
        s_out = [sem(f"out_stored{i}") for i in range(CT)]

        lora_tiles = []
        for which in range(2):
            for d in range(DT):
                for c0 in range(0, FH, 512):
                    n = min(512, FH - c0)
                    lora_tiles.append((which * D + d * P, which * FH + c0, n, which * GU + d * FH + c0))
        for h in range(HT):
            lora_tiles.append((2 * D + h * P, 2 * FH, D, 2 * GU + h * D))

        def gate_w(w, d, h, n):
            return w[:, d * FH + h * P:d * FH + h * P + n]

        def up_w(w, d, h, n):
            return w[:, GU + d * FH + h * P:GU + d * FH + h * P + n]

        def down_w(w, h, n):
            return w[0:n, 2 * GU + h * D:2 * GU + (h + 1) * D]

        def rows_of(h):
            return min(P, FH - h * P)

        USES = [("G", h, h % 2) for h in range(8)] + [("O", 0, 0), ("O", 1, 1)] \
            + [("G", 8, 0), ("G", 9, 1), ("G", 10, 0), ("T", 0, 1), ("T", 1, 0)]
        LAST_USES = [u for u in USES if u[0] == "G"]
        PER = len(USES)
        AHEAD = 4

        def use_index(c, k):
            return AHEAD + PER * c + k

        def lora_bank(n):
            return 4 + n % 4

        def lora_kept(n):
            k = 3 * (n // 4) + n % 4 + 1
            return (s_lev[1], n // 4 + 1) if n % 4 == 3 else (s_lev[0], k)

        LORA_TILES = len(lora_tiles)
        LORA_KEPT = [sum(n % 4 != 3 for n in range(LORA_TILES)), LORA_TILES // 4]
        BESIDE_PROJECT = range(-LEAD, -LEAD + 4)
        BESIDE_V = range(-LEAD + 4, -LEAD + 8)
        BESIDE_LORA = range(-LEAD + 8, 0)
        GROUP = -(-LORA_TILES // len(BESIDE_LORA))

        def lora_group(r):
            first = GROUP * (r - BESIDE_LORA[0])
            return range(first, min(LORA_TILES, first + GROUP))

        def slot(i, part):
            return bank[4 + 2 * i + part]

        block = ctx.enter_context(nc.Block())

        def hidden_read(engine, c, h):
            if h == 0:
                if not isinstance(c, int) or c > 0:
                    engine.wait_ge(s_accr, CT * c)
            elif h > 1:
                engine.wait_ge(s_down, (HT - 1) * c + h - 1)

        @block.sync
        def _(sp):
            def load_x(c, j):
                if c:
                    sp.wait_ge(s_z, CT * (c - 1) + j + 1)
                t = CT * c + j
                sp.dma_start(xin[:, j, :], x[t * P:(t + 1) * P, :]).then_inc(s_x[j], 16)

            for j in range(CT):
                load_x(0, j)
            sp.dma_start(w_raw[:, :, 0:D], w_q.rearrange("(t p) n -> p t n", p=P)).then_inc(s_w, 16)
            sp.dma_start(w_raw[:, :, D:D + KVD], w_k.rearrange("(t p) n -> p t n", p=P)).then_inc(s_w, 16)
            sp.dma_start(w_raw[:, :, D + KVD:D + 2 * KVD],
                         w_v.rearrange("(t p) n -> p t n", p=P)).then_inc(s_w, 16)
            for j in range(CT):
                load_x(1, j)
            sp.dma_start(w_raw[:, :, D + 2 * KVD:2 * D + 2 * KVD],
                         w_o.rearrange("(t p) n -> p t n", p=P)).then_inc(s_wor, 16)
            sp.wait_ge(s_zero, 2)
            for quad in range(4):
                sp.dma_start(la_raw[32 * quad:32 * quad + RANK, :], lora_a).then_inc(s_lora, 16)
                sp.dma_start(lb_raw[32 * quad:32 * quad + RANK, :], lora_b).then_inc(s_lora, 16)

            def load_q(i, r):
                row = (4 * i + r) * 2 * HD
                for s, part in enumerate(Q_PARTS):
                    sp.dma_start(qaug[r % 4][HD * s:HD * (s + 1), :, :],
                                 qs[part, bass.ds(row, 2 * HD), :].rearrange("(h d) n -> d h n", d=HD))\
                      .then_inc(s_q[r % 4], 16)

            def load_k(i, r):
                row = (2 * i + r) * HD
                for s, part in enumerate(K_PARTS):
                    sp.dma_start(kaug[r % 2][HD * s:HD * (s + 1), :], ks[part, bass.ds(row, HD), :])\
                      .then_inc(s_k[r % 2], 16)

            for j in range(CT):
                load_x(2, j)
            for c in range(CHUNKS):
                b, h = c // 2, c % 2
                if c == CHUNKS - 1:
                    sp.wait_ge(s_qst[0], 16 * 3 * c)
                    sp.wait_ge(s_qst[1], 16 * 2 * c)
                    sp.wait_ge(s_proj, 6 * c)
                    load_k(0, 0)
                    for r in range(2):
                        load_q(0, r)
                for m in range(5):
                    sp.wait_ge(s_q3, 5 * c + m + 1)
                    dst = (qs[:, b * D + m * P:b * D + (m + 1) * P, h * CHUNK:(h + 1) * CHUNK] if m < 4
                           else ks[:, b * KVD:(b + 1) * KVD, h * CHUNK:(h + 1) * CHUNK])
                    sp.dma_start(dst.rearrange("t p n -> p t n"), qp[m % 2][:, :, :]).then_inc(s_qst[m % 2], 16)
                    if m == 3 and c + 3 < CHUNKS:
                        for j in range(CT):
                            load_x(c + 3, j)

            def load_piece(i, r):
                sp.dma_start(stage[r % 2][:, :], w_ffn[:, bass.ds((4 * i + r) * PIECE, PIECE)])\
                  .then_inc(s_stage[r % 2], 16)

            def place_max(i, r):
                last = isinstance(i, int) and 4 * i + r == PAIRS - 1
                sp.wait_ge(s_mred, EVENTS if last else 68 * i + 17 * r + 21)
                for part in range(PARTS):
                    sp.dma_start(qaug[r % 4][QROWS + part:QROWS + part + 1, :, :],
                                 mturned[r % 2][MAXUNITS * part:MAXUNITS * (part + 1), :])\
                      .then_inc(s_mrow[r % 2], 16)

            def store_o(i, r):
                sp.wait_ge(s_ev, 4 * i + r + 1)
                sp.dma_start(os_[bass.ds((4 * i + r) * P, P), :], o_raw[r % 2][:, :]).then_inc(s_od[r % 2], 16)

            sp.wait_ge(s_qst[0], 16 * 3 * CHUNKS)
            sp.wait_ge(s_qst[1], 16 * 2 * CHUNKS)
            load_k(0, 1)
            for r in range(2, 4):
                load_q(0, r)
            for r in range(2):
                load_piece(0, r)
            place_max(0, 0)

            sum_rows = os_.rearrange("(r k) n -> r k n", k=32)
            o_rows = os_.rearrange("(g h r) n -> g h r n", h=2, r=32)
            inv_rows = rs.rearrange("(g h) n -> g h n", h=2)

            def load_sums(i):
                sp.wait_ge(s_od[0], 32 * (i + 1))
                sp.wait_ge(s_od[1], 32 * (i + 1))
                sp.dma_start(sums[:, :], sum_rows[bass.ds(16 * i, 16), HD, :]).then_inc(s_sum, 16)

            def store_inverted(i):
                sp.wait_ge(s_inv, i + 1)
                sp.dma_start(rs[bass.ds(16 * i, 16), :], sums[:, :]).then_inc(s_rst, 16)

            def inverted_stored(i):
                sp.wait_ge(s_rst, 16 * (i + 1))

            def load_o(c):
                b, h = c // 2, c % 2
                if c == 1:
                    sp.wait_ge(s_full, 2)
                if c > 1:
                    sp.wait_ge(s_full, use_index(c - 2, 9) + 1)
                for kk in range(DT):
                    g = b * HEADS + kk * 8
                    sp.dma_start(o_in[:, kk, :], o_rows[g:g + 8, h, 0:HD, :]).then_inc(s_oc[kk], 16)
                    sp.dma_start(den[:, kk, :], inv_rows[g:g + 8, h:h + 1, :].broadcast_to((8, HD, CHUNK)))\
                      .then_inc(s_oc[kk], 16)

            def load_xz(c):
                if c:
                    sp.wait_ge(s_full, use_index(c - 1, 0))
                sp.dma_start(xz[:, :, :], x[c * CHUNK:(c + 1) * CHUNK, :].rearrange("(j p) n -> p j n", p=P))\
                  .then_inc(s_xz, 16)

            def store_x2(c):
                sp.wait_ge(s_free, 2 if c == 0 else use_index(c - 1, 9) + 1)
                sp.dma_start(x2s[c], xz[:, :, :].rearrange("p j n -> p (j n)")).then_inc(s_x2st, 16)

            def turn(i, last):
                first = isinstance(i, int) and i == 0
                for r in range(4):
                    if not (last and r == 3):
                        place_max(i, r + 1)
                    if not (last and r >= 2):
                        sp.wait_ge(s_wadd, 4 * i + r + 1)
                        load_piece(i, r + 2)
                    if not last:
                        sp.wait_ge(s_score, 4 * KT * (4 * i + r + 1))
                        load_q(i, r + 4)
                        if r % 2:
                            load_k(i, r // 2 + 2)
                    if last and r == 2:
                        sp.wait_ge(s_wadd, PAIRS)
                        load_xz(0)
                    if last and r == 3:
                        store_x2(0)
                    if r == 3 and not first:
                        inverted_stored(i - 1)
                    store_o(i, r)
                    if last and r == 1:
                        sp.wait_ge(s_v, 2 * TURNS)
                        load_o(0)
                    if r == 0 and not first:
                        load_sums(i - 1)
                    if r == 2 and not first:
                        store_inverted(i - 1)

            turn(0, False)
            with sp.Fori(1, TURNS - 1) as i:
                turn(i, False)
            turn(TURNS - 1, True)

            load_sums(TURNS - 1)
            store_inverted(TURNS - 1)
            sp.wait_ge(s_pv, STEPS)

            def load_x2(c):
                if c == 0:
                    sp.wait_ge(s_x2st, 16)
                for j in range(CT):
                    if c:
                        sp.wait_ge(s_out[j], 16 * c)
                    sp.dma_start(x2[j][:, :], x2s[c, :, j * D:(j + 1) * D]).then_inc(s_x2l[j], 16)

            for c in range(CHUNKS):
                load_x2(c)
                if c + 1 < CHUNKS:
                    load_xz(c + 1)
                    if c == 0:
                        inverted_stored(TURNS - 1)
                    load_o(c + 1)
                    store_x2(c + 1)
                for j in range(CT):
                    sp.wait_ge(s_acc, CT * c + j + 1)
                    t = CT * c + j
                    sp.dma_start(out[t * P:(t + 1) * P, :], x2[j][:, :]).then_inc(s_out[j], 16)
            for j in range(CT):
                sp.wait_ge(s_out[j], 16 * CHUNKS)

        @block.gpsimd
        def _(pool):
            pool.memset(ident[:, :], 0.0).then_inc(s_const, 1)
            pool.memset(ident_b[:, :], 0.0).then_inc(s_const, 1)
            pool.memset(eps[:, :], EPS).then_inc(s_const, 1)
            pool.wait_ge(s_const, 3)
            for t in (ident, ident_b):
                pool.affine_select(out=t[:, :], in_=t[:, :], compare_op=ALU.not_equal, fill=1.0, base=0,
                                   pattern=[[-1, P]], channel_multiplier=1).then_inc(s_const, 1)
            pool.memset(la_raw[:, :], 0.0).then_inc(s_zero, 1)
            pool.memset(lb_raw[:, :], 0.0).then_inc(s_zero, 1)
            pool.wait_ge(s_wor, 16)
            wo_raw = w_raw[:, :, D + 2 * KVD:2 * D + 2 * KVD]
            pool.tensor_scalar(wo_hi[:, :, :], wo_raw, 1.0, None, ALU.mult).then_inc(s_wo, 1)
            pool.wait_ge(s_wo, 1)
            pool.tensor_tensor(wo_lo[:, :, :], wo_raw, wo_hi[:, :, :], ALU.subtract).then_inc(s_wo, 1)
            pool.wait_ge(s_lora, 16 * 8)
            pool.tensor_copy(la[:, :], la_raw[:, :]).then_inc(s_la, 1)
            pool.tensor_copy(lb[:, :], lb_raw[:, :]).then_inc(s_la, 1)
            for n, (t, raw, q0, q1) in enumerate(((la, la_raw, 2, 4), (lb, lb_raw, 1, 2), (lb, lb_raw, 3, 4))):
                rows = slice(32 * q0, 32 * q1)
                pool.wait_ge(s_la, n + 2)
                pool.tensor_tensor(t[rows, :], raw[rows, :], t[rows, :], ALU.subtract).then_inc(s_la, 1)
            pool.wait_ge(s_la, 5)

            def split_max(i, r):
                par = r % 2
                n = 4 * i + r
                step = 4 * n
                parts = [mparts[par][:, MAXUNITS * k:MAXUNITS * (k + 1)] for k in range(PARTS)]
                if not isinstance(i, int) or n > 0:
                    pool.wait_ge(s_wadd, n)
                if not isinstance(i, int) or n > 1:
                    pool.wait_ge(s_wh, n - 1)
                    pool.wait_ge(s_max, 68 * i + 17 * (r - 2) + 21)
                pool.wait_ge(s_mred, 68 * i + 17 * r + 16)
                pool.tensor_tensor(parts[0], negmax[par][:, :], ones[:, :], ALU.mult).then_inc(s_pp, 1)
                pool.wait_ge(s_pp, step + 1)
                pool.tensor_tensor(mres[:, 0, :], negmax[par][:, :], parts[0], ALU.subtract).then_inc(s_pp, 1)
                pool.wait_ge(s_pp, step + 2)
                pool.tensor_tensor(parts[1], mres[:, 0, :], ones[:, :], ALU.mult).then_inc(s_pp, 1)
                pool.wait_ge(s_pp, step + 3)
                pool.tensor_tensor(mres[:, 1, :], mres[:, 0, :], parts[1], ALU.subtract).then_inc(s_pp, 1)
                pool.wait_ge(s_pp, step + 4)
                pool.tensor_tensor(parts[2], mres[:, 1, :], ones[:, :], ALU.mult).then_inc(s_split, 1)

            def place_v(i, r):
                if not isinstance(i, int) or i > 0 or r >= 2:
                    pool.wait_ge(s_pv, 2 * KT * (2 * i + r - 1))
                pool.tensor_copy(v_cur[r % 2][:, :, 0:HD],
                                 v_all[:, bass.ds((2 * i + r) * KT * HD, KT * HD)]
                                 .rearrange("p (k d) -> p k d", d=HD)).then_inc(s_v, 1)

            def add_lora(n, par, staged):
                cols = bass.ds(n * PIECE, PIECE)
                pool.wait_ge(s_stage[par], staged)
                pool.tensor_tensor(w_sum[:, cols], w_sum[:, cols], stage[par][:, :], ALU.add)\
                    .then_inc(s_wadd, 1)

            def high_weights(n):
                cols = bass.ds(n * PIECE, PIECE)
                pool.tensor_copy(w_hi[:, cols], w_sum[:, cols]).then_inc(s_wh, 1)

            def low_weights(n):
                cols = bass.ds(n * PIECE, PIECE)
                pool.tensor_tensor(w_lo[:, cols], w_sum[:, cols], w_hi[:, cols], ALU.subtract)\
                    .then_inc(s_wl, 1)

            def prepare_pieces(i, r):
                n = 4 * i + r
                add_lora(n, r % 2, 16 * (2 * i + r // 2 + 1))
                if not isinstance(i, int) or n >= 1:
                    high_weights(n - 1)
                if not isinstance(i, int) or n >= 2:
                    low_weights(n - 2)

            pool.wait_ge(s_ones, 7)

            def turn(i):
                for r in range(4):
                    split_max(i, r)
                    if isinstance(i, int) and i == 0 and r == 0:
                        pool.wait_ge(s_vev, CHUNKS)
                        pool.wait_ge(s_lev[0], LORA_KEPT[0])
                        pool.wait_ge(s_lev[1], LORA_KEPT[1])
                    if r % 2 == 0:
                        place_v(i, r // 2)
                    prepare_pieces(i, r)

            turn(0)
            with pool.Fori(1, TURNS) as i:
                turn(i)
            pool.wait_ge(s_wadd, PAIRS)
            high_weights(PAIRS - 1)
            pool.wait_ge(s_wh, PAIRS - 1)
            low_weights(PAIRS - 2)
            pool.wait_ge(s_wh, PAIRS)
            low_weights(PAIRS - 1)

            def norm_o(c):
                for kk in range(DT):
                    pool.wait_ge(s_oc[kk], 32 * (c + 1))
                    pool.tensor_tensor(o_in[:, kk, :], o_in[:, kk, :], den[:, kk, :], ALU.mult).then_inc(s_on, 1)
                    pool.wait_ge(s_oh, DT * c + kk + 1)
                    pool.tensor_tensor(ol[:, kk, :], o_in[:, kk, :], oh[:, kk, :], ALU.subtract).then_inc(s_ol, 1)

            with pool.Fori(1, CHUNKS) as c:
                norm_o(c)

        @block.scalar
        def _(a):
            def std_of(c, stds, count):
                a.wait_ge(count, CT * (c + 1))
                a.activation(std[:, :], mv[:, :, 1], ACT.Sqrt, bias=eps[:, 0:1]).then_inc(stds, 1)

            a.wait_ge(s_const, 3)
            std_of(0, s_sd, s_mv)
            a.wait_ge(s_w, 48)
            a.activation(wp_hi[:, :, :], w_raw[:, :, 0:D + 2 * KVD], ACT.Copy).then_inc(s_whi, 1)

            def high_rows(c):
                for d in range(DT):
                    a.wait_ge(s_tr, DT * c + d + 1)
                    a.activation(zh[(c + 1) % 2][:, d, :], bank[d], ACT.Copy).then_inc(s_zh, 1)

            high_rows(0)
            std_of(1, s_sd, s_mv)
            for c in range(CHUNKS):
                for m in range(5):
                    n = 5 * c + m
                    a.wait_ge(s_proj, 6 * c + m + 1)
                    if n >= 2:
                        done = 3 * c + m // 2 if m % 2 == 0 else 2 * c + m // 2
                        if done:
                            a.wait_ge(s_qst[m % 2], 16 * done)
                    a.activation(qp[m % 2][:, 0, :], bank[(4, 5, 6, 7, 4)[m]], ACT.Copy).then_inc(s_q1, 1)
                    a.wait_ge(s_res, n + 1)
                    a.activation(qp[m % 2][:, 1, :], res[n % 2][:, :], ACT.Copy).then_inc(s_q2, 1)
                    if m == TURN_BEHIND and c + 1 < CHUNKS:
                        high_rows(c + 1)
                        if c + 2 < CHUNKS:
                            std_of(c + 2, s_sd, s_mv)
                a.wait_ge(s_proj, 6 * c + 6)
                b, h = c // 2, c % 2
                kept = v_all[:, :].rearrange("p (b k t d) -> p b k t d", b=BATCH, k=KV_HEADS, t=KT)
                a.activation(kept[:, b, :, CT * h:CT * (h + 1), :],
                             bank[5].rearrange("p (t k d) -> p k t d", t=CT, k=KV_HEADS), ACT.Copy)\
                    .then_inc(s_vev, 1)

            a.wait_ge(s_wo, 2)
            a.wait_ge(s_wlo, 1)
            a.wait_ge(s_la, 5)
            for n in range(LORA_TILES):
                if n % 4 != 3:
                    _, _, cols, at0 = lora_tiles[n]
                    a.wait_ge(s_lp, n + 1)
                    a.activation(w_sum[:, at0:at0 + cols], bank[lora_bank(n)][:, 0:cols], ACT.Copy)\
                        .then_inc(s_lev[0], 1)

            def exp_tile(i, r, s):
                t = TURN * i + r
                a.wait_ge(s_score, 4 * t + s + 1)
                if s == 0 and r >= 2:
                    a.wait_ge(s_pv, t - 1)
                a.activation(probs[(r % 2) * 4 + s][:, :], bank[SBANK[s]], ACT.Exp, scale=SCALE)\
                    .then_inc(s_exp, 1)

            def keep_o(i, r):
                a.wait_ge(s_pv, KT * (4 * i + r + 1))
                if not isinstance(i, int) or 2 * i + r // 2 > 0:
                    a.wait_ge(s_od[r % 2], 16 * (2 * i + r // 2))
                a.activation(o_raw[r % 2][:, :], bank[PVBANK], ACT.Copy).then_inc(s_ev, 1)

            def step(i, r):
                for s in range(4):
                    exp_tile(i, r, s)
                    if s == 1 and r % KT == 1 and r >= KT:
                        keep_o(i, r // KT - 1)

            for r in range(TURN + 2):
                step(0, r)
            with a.Fori(1, TURNS - 1) as i:
                for r in range(2, TURN + 2):
                    step(i, r)
            for r in range(2, TURN):
                step(TURNS - 1, r)
                if r == STD_STEP:
                    std_of(0, s_sd2, s_mv2)

            def high_o(c, kk):
                n = DT * c + kk
                a.wait_ge(s_on, n + 1)
                a.activation(oh[:, kk, :], o_in[:, kk, :], ACT.Copy).then_inc(s_oh, 1)

            def turned(c, part, k, i):
                a.wait_ge(s_full, k + 1)
                for q in range(2):
                    a.activation(z2h[:, 2 * part + q, :], slot(i, q), ACT.Copy).then_inc(s_zh2, 1)

            def gate(c, h, k, i):
                n = HT * c + h
                rows = rows_of(h)
                a.wait_ge(s_full, k + 1)
                if not (isinstance(c, int) and c == 0 and h < 2):
                    a.wait_ge(s_hl, n if h == 0 else n - 1)
                a.activation(act[h % 2][0:rows, :], slot(i, 0)[0:rows, :], ACT.Silu).then_inc(s_silu, 1)
                a.wait_ge(s_free, k + 1)
                hidden_read(a, c, h)
                a.activation(hh[h % 2][0:rows, :], act[h % 2][0:rows, :], ACT.Copy).then_inc(s_hh, 1)

            turned(0, 0, 2, -2)
            turned(0, 1, 3, -1)
            keep_o(TURNS - 1, 3)

            def chunk(c, last):
                k = 0
                for what, n, i in (LAST_USES if last else USES):
                    at_k = use_index(c, k)
                    if what == "G":
                        gate(c, n, at_k, i)
                        if not last and 1 <= n <= DT:
                            high_o(c + 1, n - 1)
                        if not last and n == 9:
                            std_of(c + 1, s_sd2, s_mv2)
                    if what == "T":
                        turned(c + 1, n, at_k, i)
                    k += 1

            chunk(0, False)
            with a.Fori(1, CHUNKS - 1) as c:
                chunk(c, False)
            chunk(CHUNKS - 1, True)

        @block.vector
        def _(v):
            def stats_of(j, src, loaded, count, stat):
                v.wait_ge(loaded, count)
                v.bn_stats(stats[:, j, :], src[:, j, :]).then_inc(stat, 1)

            def rstd_of(c, stds, rstds):
                v.wait_ge(stds, c + 1)
                v.reciprocal(rstd[:, :], std[:, :]).then_inc(rstds, 1)
                v.wait_ge(rstds, c + 1)

            def mean_var(c):
                for j in range(CT):
                    stats_of(j, xin, s_x[j], 16 * (c + 1), s_st)
                v.wait_ge(s_st, CT * (c + 1))
                for j in range(CT):
                    v.bn_aggr(mv[:, j, :], stats[:, j, :]).then_inc(s_mv, 1)

            def norm(c):
                rstd_of(c, s_sd, s_rs)
                if c:
                    v.wait_ge(s_tr, DT * c)
                for j in range(CT):
                    v.tensor_scalar(z[:, j, :], xin[:, j, :], mv[:, j, 0:1], rstd[:, j:j + 1],
                                    ALU.subtract, ALU.mult).then_inc(s_z, 1)

            def low_rows(c):
                for d in range(DT):
                    v.wait_ge(s_zh, DT * c + d + 1)
                    v.tensor_tensor(zl[(c + 1) % 2][:, d, :], bank[d], zh[(c + 1) % 2][:, d, :], ALU.subtract)\
                        .then_inc(s_zl, 1)

            def max_step(i, r, units, turned):
                e = events_before(i, r)
                for q in range(units):
                    u = 2 * (r + LEAD) + q
                    pair, unit = u // MAXUNITS, u % MAXUNITS
                    if unit == 0 and (pair >= 2 or not isinstance(i, int) or i > 0):
                        v.wait_ge(s_split, 4 * i + pair - 1)
                    v.wait_ge(s_max, 68 * i + e + q + 1)
                    v.tensor_reduce(negmax[pair % 2][:, unit:unit + 1], maxslot[(e + q) % 2], AX_X, ALU.max,
                                    negate=True).then_inc(s_mred, 1)
                if turned:
                    e += units
                    pair = r // KT + 1
                    v.wait_ge(s_max, 68 * i + e + 1)
                    if not isinstance(i, int) or 2 * i + pair // 2 > 0:
                        v.wait_ge(s_mrow[pair % 2], 16 * PARTS * (2 * i + pair // 2))
                    v.tensor_copy(mturned[pair % 2][:, :],
                                  maxslot[e % 2][0:PARTS * MAXUNITS, 0:P // 2].bitcast(BF16))\
                        .then_inc(s_mred, 1)

            mean_var(0)
            for i in range(2):
                v.memset(kaug[i][QROWS:KROWS, :], 1.0).then_inc(s_ones, 1)
                v.memset(v_cur[i][:, :, :], 1.0).then_inc(s_ones, 1)
                v.memset(mparts[i][:, :], 0.0).then_inc(s_ones, 1)
            v.memset(ones[:, :], 1.0).then_inc(s_ones, 1)
            norm(0)
            v.wait_ge(s_whi, 1)
            v.tensor_tensor(wp_lo[:, :, :], w_raw[:, :, 0:D + 2 * KVD], wp_hi[:, :, :], ALU.subtract)\
                .then_inc(s_wlo, 1)
            low_rows(0)
            mean_var(1)
            norm(1)

            for c in range(CHUNKS):
                for m in range(5):
                    n = 5 * c + m
                    v.wait_ge(s_q1, n + 1)
                    if n >= 2:
                        v.wait_ge(s_q2, n - 1)
                        v.wait_ge(s_q3, n - 1)
                    v.tensor_tensor(res[n % 2][:, :], bank[(4, 5, 6, 7, 4)[m]], qp[m % 2][:, 0, :], ALU.subtract)\
                        .then_inc(s_res, 1)
                    v.wait_ge(s_q2, n + 1)
                    v.tensor_tensor(qp[m % 2][:, 2, :], res[n % 2][:, :], qp[m % 2][:, 1, :], ALU.subtract)\
                        .then_inc(s_q3, 1)
                    if m == 1 and c + 2 < CHUNKS:
                        mean_var(c + 2)
                    if m == TURN_BEHIND and c + 1 < CHUNKS:
                        low_rows(c + 1)
                        if c + 2 < CHUNKS:
                            norm(c + 2)
                    if m and c == CHUNKS - 1:
                        max_step(0, BESIDE_PROJECT[m - 1], 2, False)
            for r in BESIDE_V:
                max_step(0, r, 2, False)
            v.wait_ge(s_wo, 2)
            v.wait_ge(s_la, 5)
            for r in BESIDE_LORA:
                max_step(0, r, 2, r % KT == T_STEP)
                for n in lora_group(r):
                    if n % 4 == 3:
                        _, _, cols, at0 = lora_tiles[n]
                        v.wait_ge(s_lp, n + 1)
                        v.tensor_copy(w_sum[:, at0:at0 + cols], bank[lora_bank(n)][:, 0:cols])\
                            .then_inc(s_lev[1], 1)

            def units_in(i, r):
                return 2 if i < TURNS - 1 or r < TURN - LEAD else 0

            def invert(i):
                v.wait_ge(s_sum, 16 * (i + 1))
                v.reciprocal(sums[:, :], sums[:, :]).then_inc(s_inv, 1)

            for r in range(TURN):
                max_step(0, r, 2, r % KT == T_STEP)
            with v.Fori(1, TURNS - 1) as i:
                for r in range(TURN):
                    max_step(i, r, 2, r % KT == T_STEP)
                    if r == INVERT_STEP:
                        invert(i - 1)
            for r in range(TURN):
                max_step(TURNS - 1, r, units_in(TURNS - 1, r), r % KT == T_STEP and r < TURN - KT)
                if r == INVERT_STEP:
                    invert(TURNS - 2)

            for kk in range(DT):
                v.wait_ge(s_oc[kk], 32)
                v.tensor_tensor(o_in[:, kk, :], o_in[:, kk, :], den[:, kk, :], ALU.mult).then_inc(s_on, 1)
                v.wait_ge(s_on, kk + 1)
                v.tensor_copy(oh[:, kk, :], o_in[:, kk, :]).then_inc(s_oh, 1)
                v.wait_ge(s_oh, kk + 1)
                v.tensor_tensor(ol[:, kk, :], o_in[:, kk, :], oh[:, kk, :], ALU.subtract).then_inc(s_ol, 1)

            def add_x(c, part, k, i):
                v.wait_ge(s_full, k + 1)
                if part == 0:
                    v.wait_ge(s_xz, 16 * (c + 1))
                else:
                    v.wait_ge(s_st2, CT * c + 2)
                for q in range(2):
                    j = 2 * part + q
                    v.tensor_tensor(xz[:, j, :], slot(i, q), xz[:, j, :], ALU.add)\
                        .then_inc((s_add, s_free)[q], 1)
                if part == 1:
                    mean_of(0)
                stats_of(2 * part, xz, s_add, 2 * c + part + 1, s_st2)
                stats_of(2 * part + 1, xz, s_free, k + 1, s_st2)

            def mean_of(part):
                for j in (2 * part, 2 * part + 1):
                    v.bn_aggr(mv[:, j, :], stats[:, j, :]).then_inc(s_mv2, 1)

            def norm2(c):
                rstd_of(c, s_sd2, s_rs2)
                v.wait_ge(s_x2st, 16 * (c + 1))
                for j in range(CT):
                    v.tensor_scalar(xz[:, j, :], xz[:, j, :], mv[:, j, 0:1], rstd[:, j:j + 1],
                                    ALU.subtract, ALU.mult).then_inc(s_z2, 1)

            def low_turned(c, part, i):
                for q in range(2):
                    v.wait_ge(s_zh2, DT * c + 2 * part + q + 1)
                    v.tensor_tensor(z2l[:, 2 * part + q, :], slot(i, q), z2h[:, 2 * part + q, :],
                                    ALU.subtract).then_inc((s_zl2, s_free)[q], 1)

            def hidden(c, h, k, i, means):
                n = HT * c + h
                rows = rows_of(h)
                if means:
                    v.wait_ge(s_st2, CT * (c + 2))
                v.wait_ge(s_silu, n + 1)
                v.tensor_tensor(act[h % 2][0:rows, :], slot(i, 1)[0:rows, :], act[h % 2][0:rows, :],
                                ALU.mult).then_inc(s_free, 1)
                if means:
                    mean_of(1)
                v.wait_ge(s_hh, n + 1)
                hidden_read(v, c, h)
                v.tensor_tensor(hl[h % 2][0:rows, :], act[h % 2][0:rows, :], hh[h % 2][0:rows, :],
                                ALU.subtract).then_inc(s_hl, 1)

            def add_out(c):
                for j in range(CT):
                    v.wait_ge(s_accr, CT * c + j + 1)
                    v.wait_ge(s_x2l[j], 16 * (c + 1))
                    v.tensor_tensor(x2[j][:, :], bank[j], x2[j][:, :], ALU.add).then_inc(s_acc, 1)

            add_x(0, 0, 0, -2)
            add_x(0, 1, 1, -1)
            v.wait_ge(s_st2, CT)
            mean_of(1)
            norm2(0)
            v.wait_ge(s_pv, STEPS)
            low_turned(0, 0, -2)
            low_turned(0, 1, -1)
            invert(TURNS - 1)

            def chunk(c, last):
                k = 0
                for what, n, i in (LAST_USES if last else USES):
                    at_k = use_index(c, k)
                    if what == "G":
                        hidden(c, n, at_k, i, not last and n == 8)
                        if not last and n == 9:
                            norm2(c + 1)
                    if what == "O":
                        add_x(c + 1, n, at_k, i)
                    if what == "T":
                        low_turned(c + 1, n, i)
                    k += 1
                add_out(c)

            chunk(0, False)
            with v.Fori(1, CHUNKS - 1) as c:
                chunk(c, False)
            chunk(CHUNKS - 1, True)

        @block.tensor
        def _(pe):
            def product(dst, lhs, rhs, first, last):
                n = len(lhs)
                for t, ((lh, ll), (rh, rl)) in enumerate(zip(lhs, rhs)):
                    pe.matmul(dst, lh, rh, start=first and t == 0, stop=False)
                    pe.matmul(dst, ll, rh, start=False, stop=False)
                    ins = pe.matmul(dst, lh, rl, start=False, stop=last and t == n - 1)
                return ins

            def turn_rows(c):
                if not isinstance(c, int) or c > 0:
                    pe.wait_ge(s_zl, DT * c)
                for j in range(CT):
                    pe.wait_ge(s_z, CT * c + j + 1)
                    for d in range(DT):
                        ins = pe.transpose(bank[d][:, j * P:(j + 1) * P], z[:, j, d * P:(d + 1) * P],
                                           ident[:, :])
                        if j == CT - 1:
                            ins.then_inc(s_tr, 1)

            def max_unit(i, r, q, half):
                e = events_before(i, r) + q
                u = 2 * (r + LEAD) + q
                pair, unit = u // MAXUNITS, u % MAXUNITS
                if unit == 0 and half == 0:
                    pe.wait_ge(s_q[pair % 4], 16 * 6 * (i + pair // 4 + 1))
                    if pair % 2 == 0:
                        pe.wait_ge(s_k[pair // 2 % 2], 16 * 6 * (i + pair // 4 + 1))
                if half == 0 and (not isinstance(i, int) or 68 * i + e >= 2):
                    pe.wait_ge(s_mred, 68 * i + e - 1)
                head, qt = unit // KT, unit % KT
                ins = pe.matmul(maxslot[e % 2][:, half * 512:(half + 1) * 512],
                                qaug[pair % 4][0:QROWS, head, qt * P:(qt + 1) * P],
                                kaug[pair // 2 % 2][0:QROWS, half * 512:(half + 1) * 512],
                                start=True, stop=True)
                if half:
                    ins.then_inc(s_max, 1)

            def turn_max(i, r, units):
                e = events_before(i, r) + units
                pair = r // KT + 1
                pe.wait_ge(s_split, 4 * i + pair + 1)
                pe.wait_ge(s_mred, 68 * i + e - 1)
                pe.transpose(maxslot[e % 2][:, 0:P // 2].bitcast(BF16),
                             mparts[pair % 2][:, :], ident_b[:, :]).then_inc(s_max, 1)

            def max_units(r):
                for q in range(2):
                    for half in range(2):
                        max_unit(0, r, q, half)

            def project(c):
                hi, lo = zh[(c + 1) % 2], zl[(c + 1) % 2]
                pe.wait_ge(s_zl, DT * (c + 1))
                for m in range(5):
                    if m == 0 and c:
                        pe.wait_ge(s_res, 5 * c)
                    if m == 1 and c:
                        pe.wait_ge(s_vev, c)
                    if m in (2, 3) and c:
                        pe.wait_ge(s_res, 5 * c - 4 + m)
                    if m == 4:
                        pe.wait_ge(s_res, 5 * c + 1)
                    w = slice(m * P, (m + 1) * P)
                    product(bank[(4, 5, 6, 7, 4)[m]],
                            [(wp_hi[:, d, w], wp_lo[:, d, w]) for d in range(DT)],
                            [(hi[:, d, :], lo[:, d, :]) for d in range(DT)], True, True).then_inc(s_proj, 1)
                    if m == TURN_BEHIND and c + 1 < CHUNKS:
                        turn_rows(c + 1)
                    if m and c == CHUNKS - 1:
                        max_units(BESIDE_PROJECT[m - 1])
                pe.wait_ge(s_res, 5 * c + 2)
                w = slice(D + KVD, D + 2 * KVD)
                for j in range(CT):
                    rows = slice(j * P, (j + 1) * P)
                    ins = product(bank[5][:, rows],
                                  [(hi[:, d, rows], lo[:, d, rows]) for d in range(DT)],
                                  [(wp_hi[:, d, w], wp_lo[:, d, w]) for d in range(DT)], True, True)
                    if j == CT - 1:
                        ins.then_inc(s_proj, 1)
                    if c == CHUNKS - 1:
                        max_units(BESIDE_V[j])

            pe.wait_ge(s_const, 5)
            turn_rows(0)
            pe.wait_ge(s_wlo, 1)
            for c in range(CHUNKS):
                project(c)

            pe.wait_ge(s_la, 5)
            pe.wait_ge(s_ones, 7)
            for r in BESIDE_LORA:
                max_units(r)
                if r % KT == T_STEP:
                    turn_max(0, r, 2)
                if r == BESIDE_LORA[0]:
                    pe.wait_ge(s_res, 5 * CHUNKS)
                    pe.wait_ge(s_vev, CHUNKS)
                for n in lora_group(r):
                    acol, bcol, cols, _ = lora_tiles[n]
                    if n >= 4:
                        pe.wait_ge(*lora_kept(n - 4))
                    pe.matmul(bank[lora_bank(n)][:, 0:cols], la[:, acol:acol + P], lb[:, bcol:bcol + cols],
                              start=True, stop=True).then_inc(s_lp, 1)

            def score(i, r, s):
                t = TURN * i + r
                pair, kt = r // KT, r % KT
                if kt == 0 and s == 0:
                    pe.wait_ge(s_mrow[pair % 2], 16 * PARTS * (2 * i + pair // 2 + 1))
                if s == 3:
                    pe.wait_ge(s_exp, 4 * t + 1)
                elif not isinstance(i, int) or t > 0:
                    pe.wait_ge(s_exp, 4 * t - (0, 2, 1)[s])
                head, half = s // 2, s % 2
                pe.matmul(bank[SBANK[s]], kaug[pair // 2 % 2][0:KROWS, kt * P:(kt + 1) * P],
                          qaug[pair % 4][0:KROWS, head, half * CHUNK:(half + 1) * CHUNK],
                          start=True, stop=True).then_inc(s_score, 1)

            def pv(i, r):
                t = TURN * i + r
                pair, kt = r // KT, r % KT
                pe.wait_ge(s_exp, 4 * t + 4)
                if kt == 0:
                    if not isinstance(i, int) or 4 * i + pair > 0:
                        pe.wait_ge(s_ev, 4 * i + pair)
                    pe.wait_ge(s_v, 2 * i + pair // 2 + 1)
                for s in range(4):
                    ins = pe.matmul(bank[PVBANK][32 * s:32 * s + 32, :], v_cur[pair // 2 % 2][:, kt, :],
                                    probs[(r % 2) * 4 + s][:, :], start=kt == 0, stop=kt == KT - 1,
                                    skip_group_check=True)
                ins.then_inc(s_pv, 1)

            def step(i, r, with_pv=True, units=2, turned=True):
                for s in range(4):
                    score(i, r, s)
                    if units:
                        max_unit(i, r, s // 2, s % 2)
                if with_pv:
                    pv(i, r - 1)
                if r % KT == T_STEP and turned:
                    turn_max(i, r, units)

            for i in range(2):
                pe.wait_ge(s_lev[i], LORA_KEPT[i])
            for r in range(TURN + 1):
                step(0, r, with_pv=r > 0)
            with pe.Fori(1, TURNS - 1) as i:
                for r in range(1, TURN + 1):
                    step(i, r)
            def free_wait(c, k):
                pe.wait_ge(s_free, use_index(c, 0) if k == 0 else use_index(c, k) - 1)

            def out_project(c, part, i):
                pe.wait_ge(s_ol, DT * (c + 1))
                for q in range(2):
                    rows = slice((2 * part + q) * P, (2 * part + q + 1) * P)
                    ins = product(slot(i, q), [(oh[:, d, rows], ol[:, d, rows]) for d in range(DT)],
                                  [(wo_hi[:, d, :], wo_lo[:, d, :]) for d in range(DT)], True, True)
                ins.then_inc(s_full, 1)

            def turn_rows2(c, part, i):
                pe.wait_ge(s_z2, CT * (c + 1))
                for q in range(2):
                    for j in range(CT):
                        d = 2 * part + q
                        ins = pe.transpose(slot(i, q)[:, j * P:(j + 1) * P], xz[:, j, d * P:(d + 1) * P],
                                           ident[:, :])
                ins.then_inc(s_full, 1)

            def gate_up(c, h, i):
                n = rows_of(h)
                for q, cols in enumerate((gate_w, up_w)):
                    ins = product(slot(i, q)[0:n, :], [(cols(w_hi, d, h, n), cols(w_lo, d, h, n)) for d in range(DT)],
                                  [(z2h[:, d, :], z2l[:, d, :]) for d in range(DT)], True, True)
                ins.then_inc(s_full, 1)

            def down(c, h):
                n = rows_of(h)
                pe.wait_ge(s_hl, HT * c + h + 1)
                if h == 0 and (not isinstance(c, int) or c > 0):
                    pe.wait_ge(s_acc, CT * c)
                for j in range(CT):
                    rows = slice(j * P, (j + 1) * P)
                    ins = product(bank[j], [(hh[h % 2][0:n, rows], hl[h % 2][0:n, rows])],
                                  [(down_w(w_hi, h, n), down_w(w_lo, h, n))], h == 0, h == HT - 1)
                    if h == HT - 1:
                        ins.then_inc(s_accr, 1)
                    elif j == CT - 1:
                        ins.then_inc(s_down, 1)

            for r in range(1, TURN):
                step(TURNS - 1, r, units=2 if r < TURN - LEAD else 0, turned=r < TURN - KT)
                if r == O_STEPS[0]:
                    pe.wait_ge(s_mred, EVENTS)
                    pe.wait_ge(s_wo, 2)
                    out_project(0, 0, -2)
                if r == O_STEPS[1]:
                    out_project(0, 1, -1)
            pe.wait_ge(s_free, 2)
            turn_rows2(0, 0, -2)
            turn_rows2(0, 1, -1)
            pv(TURNS - 1, TURN - 1)

            pe.wait_ge(s_exp, 4 * STEPS)
            pe.wait_ge(s_ev, PAIRS)
            pe.wait_ge(s_wl, PAIRS)

            def chunk(c, last):
                k = 0
                for what, n, i in (LAST_USES if last else USES):
                    free_wait(c, k)
                    if what == "G":
                        gate_up(c, n, i)
                        if n > 0:
                            down(c, n - 1)
                        if n == HT - 1:
                            down(c, n)
                    if what == "O":
                        out_project(c + 1, n, i)
                    if what == "T":
                        turn_rows2(c + 1, n, i)
                    k += 1

            chunk(0, False)
            with pe.Fori(1, CHUNKS - 1) as c:
                chunk(c, False)
            chunk(CHUNKS - 1, True)


def kernel(**inputs):
    import numpy as np
    import concourse.bacc as bacc
    from concourse.bass_utils import run_bass_kernel_spmd

    def tiles(w):
        t = -(-w.shape[0] // P)
        full = np.zeros((t * P, w.shape[1]), w.dtype)
        full[:w.shape[0]] = w
        return full.reshape(t, P, w.shape[1]).transpose(1, 0, 2).reshape(P, t * w.shape[1])

    a = {n.replace("L0_attn_", "").replace("L0_ffn_", ""): np.asarray(v) for n, v in inputs.items()}
    down_a = np.zeros((RANK, HT * P), a["down_a"].dtype)
    down_a[:, :FH] = a["down_a"]
    arrays = {
        "x": a["x"].reshape(BATCH * SEQ, D),
        "w_q": a["w_q"], "w_k": a["w_k"], "w_v": a["w_v"], "w_o": a["w_o"],
        "w_ffn": np.concatenate([tiles(a["gate_w"].T), tiles(a["up_w"].T), tiles(a["down_w"].T)], axis=1),
        "lora_a": np.concatenate([a["gate_a"], a["up_a"], down_a], axis=1),
        "lora_b": np.concatenate([a["gate_b"].T, a["up_b"].T, a["down_b"].T], axis=1),
    }
    arrays = {n: np.ascontiguousarray(v) for n, v in arrays.items()}
    nc = bacc.Bacc("TRN2", target_bir_lowering=False, num_devices=1)
    args = [nc.dram_tensor(n, v.shape, mybir.dt.from_np(v.dtype), kind="ExternalInput").ap()
            for n, v in arrays.items()]
    args += [
        nc.dram_tensor("q_parts", (PARTS, BATCH * D, SEQ), BF16).ap(),
        nc.dram_tensor("k_parts", (PARTS, BATCH * KVD, SEQ), BF16).ap(),
        nc.dram_tensor("o_sums", (PAIRS * P, CHUNK), F32).ap(),
        nc.dram_tensor("inverted_sums", (PAIRS * 4, CHUNK), F32).ap(),
        nc.dram_tensor("x_plus_attention", (CHUNKS, P, CT * D), F32).ap(),
        nc.dram_tensor("out", (BATCH * SEQ, D), F32, kind="ExternalOutput").ap(),
    ]
    build(nc, *args)
    r = run_bass_kernel_spmd(nc, [arrays], core_ids=[0])
    return r.results[0]["out"].reshape(BATCH, SEQ, D)
```

```python
from contextlib import ExitStack

import concourse.bass as bass
from concourse import mybir

ALU = mybir.AluOpType
ACT = mybir.ActivationFunctionType
F32 = mybir.dt.float32
F32R = mybir.dt.float32r
BF16 = mybir.dt.bfloat16
AX_X = mybir.AxisListType.X

P = 128
BATCH, SEQ, D = 2, 1024, 512
HEADS, KV_HEADS = 32, 8
HD = D // HEADS
KVD = HD * KV_HEADS
FH = 1376
RANK = 16
EPS = 1e-5
SCALE = HD ** -0.5

DT = D // P
CHUNK = 512
CHUNKS = BATCH * SEQ // CHUNK
CT = CHUNK // P
HT = -(-FH // P)
GU = DT * FH
WCOLS = 2 * GU + HT * D

PAIRS = BATCH * HEADS // 2
KT = SEQ // P
STEPS = PAIRS * KT
TURN = 4 * KT
TURNS = STEPS // TURN
MAXUNITS = 2 * KT
TURN_UNITS = 4 * MAXUNITS
TURN_BEHIND = 2
MEAN_BEHIND = 4
LEAD = 12
INVERT_STEP = 20
O_STEP = 22
O_PIECES = 3
STD_STEP = 28
T_BEHIND = 30
T_STEP = 5
PARTS = 3
Q_PARTS = (0, 0, 1, 0, 1, 2)
K_PARTS = (0, 1, 0, 2, 1, 0)
QROWS = HD * len(Q_PARTS)
KROWS = QROWS + PARTS
SBANK = (4, 5, 6, 4)
PVBANK = 7
PIECE = WCOLS // PAIRS
LORA_A_COLS = 2 * D + HT * P
LORA_B_COLS = 2 * FH + D


def unit_of(r, q):
    return 2 * (r + LEAD) + q


def build(nc, x, w_q, w_k, w_v, w_o, w_ffn, lora_a, lora_b, qs, ks, os_, rs, x2s, out):
    ctx = ExitStack()
    with ctx:
        def sem(name):
            return ctx.enter_context(nc.semaphore(name))

        base = -(-nc.sbuf_base // 32) * 32
        arena = ctx.enter_context(nc.sbuf_tensor("arena", [P, (nc.sbuf_usable_end - base - 64) // 4], F32))
        del arena
        cursor = [base]

        def region(start):
            cursor[0] = start

        def at(name, shape, dt):
            size = 1
            for n in shape[1:]:
                size *= n
            nbytes = size * (2 if dt == BF16 else 4)
            t = nc.alloc_sbuf_tensor_at(name, shape, dt, offset=cursor[0])
            cursor[0] += -(-nbytes // 32) * 32
            return t

        R1 = base
        region(R1)
        w_lo = at("w_lo", [P, WCOLS], F32R)
        R2 = cursor[0]
        w_hi = at("w_hi", [P, WCOLS], F32R)
        R3 = cursor[0]
        region(R1)
        w_sum = at("w_sum", [P, WCOLS], F32)
        region(R1)
        w_raw = at("w_raw", [P, DT, 2 * D + 2 * KVD], F32)
        la_raw = at("la_raw", [P, LORA_A_COLS], F32)
        lb_raw = at("lb_raw", [P, LORA_B_COLS], F32)
        region(R2)
        xin = at("xin", [P, CT, D], F32)
        z = at("z", [P, CT, D], F32)
        zh = [at("zh0", [P, DT, CHUNK], F32R)]
        zl = [at("zl0", [P, DT, CHUNK], F32R)]
        qp = [at(f"qp{i}", [P, PARTS, CHUNK], BF16) for i in range(2)]
        wp_hi = at("wp_hi", [P, DT, D + 2 * KVD], F32R)
        wp_lo = at("wp_lo", [P, DT, D + 2 * KVD], F32R)
        res = [at("res0", [P, CHUNK], F32)]
        assert cursor[0] <= R3
        region(R3)
        wo_hi = at("wo_hi", [P, DT, D], F32R)
        wo_lo = at("wo_lo", [P, DT, D], F32R)
        ident = at("ident", [P, P], F32)
        ident_b = at("ident_b", [P, P], BF16)
        stats = at("stats", [P, CT, 6], F32)
        mv = at("mv", [P, CT, 2], F32)
        std = at("std", [P, CT], F32)
        rstd = at("rstd", [P, CT], F32)
        eps = at("eps", [P, 1], F32)
        warm = at("warm", [P, 2], F32)
        sums = at("sums", [P, 8 * 2 * CHUNK // P], F32)
        R4 = cursor[0]
        v_all = at("v_all", [P, BATCH * KV_HEADS * KT * HD], F32)
        RQ = cursor[0]
        qaug = [at(f"qaug{i}", [P, 2, SEQ], BF16) for i in range(2)]
        kaug = [at("kaug0", [P, SEQ], BF16)]
        v_cur = [at("v_cur0", [P, KT, 32], F32)]
        ZROWS = cursor[0]
        stage = [at(f"stage{i}", [P, PIECE], F32) for i in range(2)]
        cursor[0] = R4 + 4 * (2 * DT * CHUNK + CT * D)
        qaug += [at(f"qaug{i}", [P, 2, SEQ], BF16) for i in range(2, 4)]
        kaug += [at("kaug1", [P, SEQ], BF16)]
        v_cur += [at("v_cur1", [P, KT, 32], F32)]
        RP = cursor[0]
        probs = [at(f"probs{i}", [P, CHUNK], F32) for i in range(8)]
        o_raw = [at(f"o_raw{i}", [P, CHUNK], F32) for i in range(2)]
        cursor[0] = max(cursor[0], RP + 4 * (LORA_A_COLS + LORA_B_COLS))
        negmax = [at(f"negmax{i}", [P, MAXUNITS], F32) for i in range(2)]
        mres = at("mres", [P, 2, MAXUNITS], F32)
        ones = at("ones", [P, MAXUNITS], F32)
        mparts = [at(f"mparts{i}", [P, P], BF16) for i in range(2)]
        mturned = [at(f"mturned{i}", [PARTS * MAXUNITS, P], BF16) for i in range(2)]
        res += [at("res1", [P, CHUNK], F32)]
        region(RP)
        la = at("la", [P, LORA_A_COLS], F32R)
        lb = at("lb", [P, LORA_B_COLS], F32R)
        region(ZROWS)
        zh += [at("zh1", [P, DT, CHUNK], F32R)]
        zl += [at("zl1", [P, DT, CHUNK], F32R)]
        assert cursor[0] <= RP
        region(R4)
        den = at("den", [P, DT, CHUNK], F32)
        o_in = at("o_in", [P, DT, CHUNK], F32)
        region(R4)
        oh = at("oh", [P, DT, CHUNK], F32R)
        ol = at("ol", [P, DT, CHUNK], F32R)
        xz = at("xz", [P, CT, D], F32)
        z2h = at("z2h", [P, DT, CHUNK], F32R)
        z2l = at("z2l", [P, DT, CHUNK], F32R)
        act = [at(f"act{i}", [P, CHUNK], F32) for i in range(2)]
        hh = [at(f"hh{i}", [P, CHUNK], F32R) for i in range(2)]
        hl = [at(f"hl{i}", [P, CHUNK], F32R) for i in range(2)]
        x2 = [at(f"x2_{i}", [P, D], F32) for i in range(CT)]

        psum = ctx.enter_context(nc.psum_tensor("psum", [P, 8 * 512], F32))
        bank = [psum[:, 512 * i:512 * (i + 1)] for i in range(8)]
        maxslot = [psum[:, 0:1024], psum[:, 1024:2048]]

        s_x = [sem(f"x_loaded{j}") for j in range(CT)]
        s_wq = sem("wq_loaded")
        s_wkv = sem("wk_wv_loaded")
        s_wor = sem("wo_loaded")
        s_lora = sem("lora_loaded")
        s_zero = sem("lora_zeroed")
        s_const = sem("constants_set")
        s_ones = sem("ones_set")
        s_ones1 = sem("second_ones_set")
        s_whi = sem("proj_weights_hi")
        s_wlo = sem("proj_weights_lo_dve")
        s_wlop = sem("proj_weights_lo_pool")
        s_wo = sem("wo_split")
        s_la = sem("lora_split")
        s_st = sem("ln_stats")
        s_mv = sem("ln_mean_var")
        s_sd = sem("ln_std")
        s_rs = sem("ln_rstd")
        s_z = sem("ln_normed")
        s_tr = sem("z_turned")
        s_zh = sem("z_hi")
        s_zl = sem("z_lo")
        s_proj = sem("projected")
        s_q1 = sem("part1")
        s_res = sem("part1_rest")
        s_q2 = sem("part2")
        s_q3 = sem("part3")
        s_vev = sem("v_kept")
        s_qst = [sem(f"qk_stored{i}") for i in range(2)]
        s_lp = sem("lora_product")
        s_lev = [sem("lora_kept_act"), sem("lora_kept_dve")]
        s_q = [sem(f"q_loaded{i}") for i in range(4)]
        s_k = [sem(f"k_loaded{i}") for i in range(2)]
        s_v = sem("v_placed")
        s_score = sem("scores")
        s_exp = sem("exps")
        s_pv = sem("pv_steps")
        s_ev = sem("o_kept")
        s_od = [sem(f"o_stored{i}") for i in range(2)]
        s_max = sem("max_scores")
        s_mred = sem("max_reduced")
        s_mturn = sem("max_turned")
        s_mrows = sem("max_turned_kept")
        s_pp = sem("max_split_steps")
        s_split = sem("max_split")
        s_mrow = [sem(f"max_rows{i}") for i in range(2)]
        s_stage = [sem(f"weights_staged{i}") for i in range(2)]
        s_wadd = sem("weights_added")
        s_wh = sem("weights_hi")
        s_wl = sem("weights_lo")
        s_sum = sem("sums_loaded")
        s_inv = sem("sums_inverted")
        s_rst = sem("inverted_stored")
        s_oc = [sem(f"o_loaded{i}") for i in range(DT)]
        s_on = sem("o_normed")
        s_oh = sem("o_hi")
        s_ol = sem("o_lo")
        s_xz = sem("x_reloaded")
        s_full = sem("ring_full")
        s_free = sem("ring_free")
        s_add = sem("x2_summed")
        s_x2st = sem("x2_stored")
        s_st2 = sem("ln2_stats")
        s_mv2 = sem("ln2_mean_var")
        s_sd2 = sem("ln2_std")
        s_rs2 = sem("ln2_rstd")
        s_z2 = sem("ln2_normed")
        s_zh2 = sem("z2_hi")
        s_silu = sem("silu")
        s_hh = sem("hidden_hi")
        s_hl = sem("hidden_lo")
        s_down = sem("down_steps")
        s_accr = sem("acc_ready")
        s_acc = sem("acc_taken")
        s_x2l = [sem(f"x2_loaded{i}") for i in range(CT)]
        s_out = [sem(f"out_stored{i}") for i in range(CT)]

        lora_tiles = []
        for which in range(2):
            for d in range(DT):
                for c0 in range(0, FH, 512):
                    n = min(512, FH - c0)
                    lora_tiles.append((which * D + d * P, which * FH + c0, n, which * GU + d * FH + c0))
        for h in range(HT):
            lora_tiles.append((2 * D + h * P, 2 * FH, D, 2 * GU + h * D))

        def gate_w(w, d, h, n):
            return w[:, d * FH + h * P:d * FH + h * P + n]

        def up_w(w, d, h, n):
            return w[:, GU + d * FH + h * P:GU + d * FH + h * P + n]

        def down_w(w, h, n):
            return w[0:n, 2 * GU + h * D:2 * GU + (h + 1) * D]

        def rows_of(h):
            return min(P, FH - h * P)

        USES = [("G", h, h % 2) for h in range(8)] + [("O", 0, 0), ("O", 1, 1)] \
            + [("G", 8, 0), ("G", 9, 1), ("G", 10, 0), ("T", 0, 1), ("T", 1, 0)]
        LAST_USES = [u for u in USES if u[0] == "G"]
        PER = len(USES)
        AHEAD = 4

        def use_index(c, k):
            return AHEAD + PER * c + k

        BESIDE = {at: r for r, at in enumerate([(2, 8)] + [(3, m) for m in range(9)], -LEAD)}
        TAIL = range(BESIDE[3, 5], 0)
        LORA_TILES = len(lora_tiles)
        LORA_IN_V = (1, 2) * CT
        LORA_EARLY = sum(LORA_IN_V)
        LORA_GROUP = -(-(LORA_TILES - LORA_EARLY) // (2 * len(TAIL) - len(LORA_IN_V)))

        def lora_group(r, q):
            k = 2 * (r - TAIL[0]) + q
            if k < len(LORA_IN_V):
                return range(sum(LORA_IN_V[:k]), sum(LORA_IN_V[:k + 1]))
            first = LORA_EARLY + LORA_GROUP * (k - len(LORA_IN_V))
            return range(first, min(LORA_TILES, first + LORA_GROUP))

        def by_dve(n):
            return n >= LORA_EARLY and n % 3 == 2

        def lora_bank(n):
            return 6 + n % 2 if n < LORA_EARLY else 4 + n % 4

        def lora_kept(n):
            return s_lev[by_dve(n)], sum(by_dve(k) == by_dve(n) for k in range(n + 1))

        LORA_KEPT = [sum(by_dve(n) == by for n in range(LORA_TILES)) for by in (False, True)]

        def slot(i, part):
            return bank[4 + 2 * i + part]

        block = ctx.enter_context(nc.Block())

        def hidden_read(engine, c, h):
            if h == 0:
                if not isinstance(c, int) or c > 0:
                    engine.wait_ge(s_accr, CT * c)
            elif h > 1:
                engine.wait_ge(s_down, (HT - 1) * c + h - 1)

        @block.sync
        def _(sp):
            def load_x(c, j):
                if c:
                    sp.wait_ge(s_z, CT * (c - 1) + j + 1)
                t = CT * c + j
                sp.dma_start(xin[:, j, :], x[t * P:(t + 1) * P, :]).then_inc(s_x[j], 16)

            for j in range(CT):
                load_x(0, j)
            sp.dma_start(w_raw[:, :, 0:D], w_q.rearrange("(t p) n -> p t n", p=P)).then_inc(s_wq, 16)
            sp.dma_start(w_raw[:, :, D:D + KVD], w_k.rearrange("(t p) n -> p t n", p=P)).then_inc(s_wkv, 16)
            sp.dma_start(w_raw[:, :, D + KVD:D + 2 * KVD],
                         w_v.rearrange("(t p) n -> p t n", p=P)).then_inc(s_wkv, 16)
            for j in range(CT):
                load_x(1, j)
            sp.dma_start(w_raw[:, :, D + 2 * KVD:2 * D + 2 * KVD],
                         w_o.rearrange("(t p) n -> p t n", p=P)).then_inc(s_wor, 16)
            sp.wait_ge(s_zero, 2)
            for quad in range(4):
                sp.dma_start(la_raw[32 * quad:32 * quad + RANK, :], lora_a).then_inc(s_lora, 16)
                sp.dma_start(lb_raw[32 * quad:32 * quad + RANK, :], lora_b).then_inc(s_lora, 16)

            def load_q(i, r):
                row = (4 * i + r) * 2 * HD
                for s, part in enumerate(Q_PARTS):
                    sp.dma_start(qaug[r % 4][HD * s:HD * (s + 1), :, :],
                                 qs[part, bass.ds(row, 2 * HD), :].rearrange("(h d) n -> d h n", d=HD))\
                      .then_inc(s_q[r % 4], 16)

            def load_k(i, r):
                row = (2 * i + r) * HD
                for s, part in enumerate(K_PARTS):
                    sp.dma_start(kaug[r % 2][HD * s:HD * (s + 1), :], ks[part, bass.ds(row, HD), :])\
                      .then_inc(s_k[r % 2], 16)

            for j in range(CT):
                load_x(2, j)
            for c in range(CHUNKS):
                b, h = c // 2, c % 2
                if c == 2:
                    sp.wait_ge(s_qst[0], 16 * 3 * c)
                    sp.wait_ge(s_qst[1], 16 * 2 * c)
                for m in range(5):
                    sp.wait_ge(s_q3, 5 * c + m + 1)
                    dst = (qs[:, b * D + m * P:b * D + (m + 1) * P, h * CHUNK:(h + 1) * CHUNK] if m < 4
                           else ks[:, b * KVD:(b + 1) * KVD, h * CHUNK:(h + 1) * CHUNK])
                    sp.dma_start(dst.rearrange("t p n -> p t n"), qp[m % 2][:, :, :]).then_inc(s_qst[m % 2], 16)
                    if m == 2 and c == 2:
                        load_q(0, 0)
                        load_k(0, 0)
                    if m == 4 and c == 2:
                        load_q(0, 1)
                    if m == 4 and c + 3 < CHUNKS:
                        for j in range(CT):
                            load_x(c + 3, j)

            def load_piece(i, r):
                sp.dma_start(stage[r % 2][:, :], w_ffn[:, bass.ds((4 * i + r) * PIECE, PIECE)])\
                  .then_inc(s_stage[r % 2], 16)

            def place_max(i, r):
                sp.wait_ge(s_mrows, 4 * i + r + 1)
                for part in range(PARTS):
                    sp.dma_start(qaug[r % 4][QROWS + part:QROWS + part + 1, :, :],
                                 mturned[r % 2][MAXUNITS * part:MAXUNITS * (part + 1), :])\
                      .then_inc(s_mrow[r % 2], 16)

            def store_o(i, r):
                sp.wait_ge(s_ev, 4 * i + r + 1)
                sp.dma_start(os_[bass.ds((4 * i + r) * P, P), :], o_raw[r % 2][:, :]).then_inc(s_od[r % 2], 16)

            sp.wait_ge(s_qst[0], 16 * 3 * CHUNKS)
            sp.wait_ge(s_qst[1], 16 * 2 * CHUNKS)
            load_k(0, 1)
            for r in range(2, 4):
                load_q(0, r)
            for r in range(2):
                load_piece(0, r)
            place_max(0, 0)

            sum_rows = os_.rearrange("(r k) n -> r k n", k=32)
            o_rows = os_.rearrange("(g h r) n -> g h r n", h=2, r=32)
            inv_rows = rs.rearrange("(g h) n -> g h n", h=2)

            def load_sums(i):
                sp.wait_ge(s_od[0], 32 * (i + 1))
                sp.wait_ge(s_od[1], 32 * (i + 1))
                sp.dma_start(sums[:, :], sum_rows[bass.ds(16 * i, 16), HD, :]).then_inc(s_sum, 16)

            def store_inverted(i):
                sp.wait_ge(s_inv, i + 1)
                sp.dma_start(rs[bass.ds(16 * i, 16), :], sums[:, :]).then_inc(s_rst, 16)

            def inverted_stored(i):
                sp.wait_ge(s_rst, 16 * (i + 1))

            def load_o(c):
                b, h = c // 2, c % 2
                if c == 1:
                    sp.wait_ge(s_full, 2)
                if c > 1:
                    sp.wait_ge(s_full, use_index(c - 2, 9) + 1)
                for kk in range(DT):
                    g = b * HEADS + kk * 8
                    sp.dma_start(o_in[:, kk, :], o_rows[g:g + 8, h, 0:HD, :]).then_inc(s_oc[kk], 16)
                    sp.dma_start(den[:, kk, :], inv_rows[g:g + 8, h:h + 1, :].broadcast_to((8, HD, CHUNK)))\
                      .then_inc(s_oc[kk], 16)

            def load_xz(c):
                if c:
                    sp.wait_ge(s_full, use_index(c - 1, 0))
                sp.dma_start(xz[:, :, :], x[c * CHUNK:(c + 1) * CHUNK, :].rearrange("(j p) n -> p j n", p=P))\
                  .then_inc(s_xz, 16)

            def store_x2(c):
                sp.wait_ge(s_free, 2 if c == 0 else use_index(c - 1, 9) + 1)
                sp.dma_start(x2s[c], xz[:, :, :].rearrange("p j n -> p (j n)")).then_inc(s_x2st, 16)

            def turn(i, last):
                first = isinstance(i, int) and i == 0
                for r in range(4):
                    if not (last and r == 3):
                        place_max(i, r + 1)
                    if not (last and r >= 2):
                        sp.wait_ge(s_wadd, 4 * i + r + 1)
                        load_piece(i, r + 2)
                    if not last:
                        sp.wait_ge(s_score, 4 * KT * (4 * i + r + 1))
                        load_q(i, r + 4)
                        if r % 2:
                            load_k(i, r // 2 + 2)
                    if last and r == 2:
                        sp.wait_ge(s_wadd, PAIRS)
                        load_xz(0)
                    if last and r == 3:
                        store_x2(0)
                    if r == 3 and not first:
                        inverted_stored(i - 1)
                    store_o(i, r)
                    if last and r == 1:
                        sp.wait_ge(s_v, 2 * TURNS)
                        load_o(0)
                    if r == 0 and not first:
                        load_sums(i - 1)
                    if r == 2 and not first:
                        store_inverted(i - 1)

            turn(0, False)
            with sp.Fori(1, TURNS - 1) as i:
                turn(i, False)
            turn(TURNS - 1, True)

            load_sums(TURNS - 1)
            store_inverted(TURNS - 1)
            sp.wait_ge(s_pv, STEPS)

            def load_x2(c):
                if c == 0:
                    sp.wait_ge(s_x2st, 16)
                for j in range(CT):
                    if c:
                        sp.wait_ge(s_out[j], 16 * c)
                    sp.dma_start(x2[j][:, :], x2s[c, :, j * D:(j + 1) * D]).then_inc(s_x2l[j], 16)

            for c in range(CHUNKS):
                load_x2(c)
                if c + 1 < CHUNKS:
                    load_xz(c + 1)
                    if c == 0:
                        inverted_stored(TURNS - 1)
                    load_o(c + 1)
                    store_x2(c + 1)
                for j in range(CT):
                    sp.wait_ge(s_acc, CT * c + j + 1)
                    t = CT * c + j
                    sp.dma_start(out[t * P:(t + 1) * P, :], x2[j][:, :]).then_inc(s_out[j], 16)
            for j in range(CT):
                sp.wait_ge(s_out[j], 16 * CHUNKS)

        @block.gpsimd
        def _(pool):
            pool.memset(ident[:, :], 0.0).then_inc(s_const, 1)
            pool.memset(ident_b[:, :], 0.0).then_inc(s_const, 1)
            pool.memset(eps[:, :], EPS).then_inc(s_const, 1)
            pool.wait_ge(s_const, 3)
            for t in (ident, ident_b):
                pool.affine_select(out=t[:, :], in_=t[:, :], compare_op=ALU.not_equal, fill=1.0, base=0,
                                   pattern=[[-1, P]], channel_multiplier=1).then_inc(s_const, 1)
            pool.memset(la_raw[:, :], 0.0).then_inc(s_zero, 1)
            pool.memset(lb_raw[:, :], 0.0).then_inc(s_zero, 1)
            pool.wait_ge(s_whi, 3)
            kv = slice(D, D + 2 * KVD)
            pool.tensor_tensor(wp_lo[:, :, kv], w_raw[:, :, kv], wp_hi[:, :, kv], ALU.subtract).then_inc(s_wlop, 1)
            pool.wait_ge(s_wlop, 1)
            pool.wait_ge(s_wor, 16)
            wo_raw = w_raw[:, :, D + 2 * KVD:2 * D + 2 * KVD]
            pool.tensor_scalar(wo_hi[:, :, :], wo_raw, 1.0, None, ALU.mult).then_inc(s_wo, 1)
            pool.wait_ge(s_wo, 1)
            pool.tensor_tensor(wo_lo[:, :, :], wo_raw, wo_hi[:, :, :], ALU.subtract).then_inc(s_wo, 1)
            pool.wait_ge(s_lora, 16 * 8)
            pool.tensor_copy(la[:, :], la_raw[:, :]).then_inc(s_la, 1)
            pool.tensor_copy(lb[:, :], lb_raw[:, :]).then_inc(s_la, 1)
            for n, (t, raw, q0, q1) in enumerate(((la, la_raw, 2, 4), (lb, lb_raw, 1, 2), (lb, lb_raw, 3, 4))):
                rows = slice(32 * q0, 32 * q1)
                pool.wait_ge(s_la, n + 2)
                pool.tensor_tensor(t[rows, :], raw[rows, :], t[rows, :], ALU.subtract).then_inc(s_la, 1)
            pool.wait_ge(s_la, 5)
            pool.wait_ge(s_proj, 6 * 3)
            pool.memset(kaug[1][QROWS:KROWS, :], 1.0).then_inc(s_ones1, 1)
            pool.wait_ge(s_ones1, 1)
            pool.memset(v_cur[1][:, :, :], 1.0).then_inc(s_ones1, 1)
            pool.wait_ge(s_ones1, 2)

            def split_max(i, r):
                par = r % 2
                n = 4 * i + r
                step = 4 * n
                parts = [mparts[par][:, MAXUNITS * k:MAXUNITS * (k + 1)] for k in range(PARTS)]
                if not isinstance(i, int) or n > 0:
                    pool.wait_ge(s_wadd, n)
                if not isinstance(i, int) or n > 1:
                    pool.wait_ge(s_wh, n - 1)
                    pool.wait_ge(s_mturn, n - 1)
                pool.wait_ge(s_mred, TURN_UNITS * i + MAXUNITS * (r + 1))
                pool.tensor_tensor(parts[0], negmax[par][:, :], ones[:, :], ALU.mult).then_inc(s_pp, 1)
                pool.wait_ge(s_pp, step + 1)
                pool.tensor_tensor(mres[:, 0, :], negmax[par][:, :], parts[0], ALU.subtract).then_inc(s_pp, 1)
                pool.wait_ge(s_pp, step + 2)
                pool.tensor_tensor(parts[1], mres[:, 0, :], ones[:, :], ALU.mult).then_inc(s_pp, 1)
                pool.wait_ge(s_pp, step + 3)
                pool.tensor_tensor(mres[:, 1, :], mres[:, 0, :], parts[1], ALU.subtract).then_inc(s_pp, 1)
                pool.wait_ge(s_pp, step + 4)
                pool.tensor_tensor(parts[2], mres[:, 1, :], ones[:, :], ALU.mult).then_inc(s_split, 1)

            def place_v(i, r):
                if not isinstance(i, int) or i > 0 or r >= 2:
                    pool.wait_ge(s_pv, 2 * KT * (2 * i + r - 1))
                pool.tensor_copy(v_cur[r % 2][:, :, 0:HD],
                                 v_all[:, bass.ds((2 * i + r) * KT * HD, KT * HD)]
                                 .rearrange("p (k d) -> p k d", d=HD)).then_inc(s_v, 1)

            def add_lora(n, par, staged):
                cols = bass.ds(n * PIECE, PIECE)
                pool.wait_ge(s_stage[par], staged)
                pool.tensor_tensor(w_sum[:, cols], w_sum[:, cols], stage[par][:, :], ALU.add)\
                    .then_inc(s_wadd, 1)

            def high_weights(n):
                cols = bass.ds(n * PIECE, PIECE)
                pool.tensor_copy(w_hi[:, cols], w_sum[:, cols]).then_inc(s_wh, 1)

            def low_weights(n):
                cols = bass.ds(n * PIECE, PIECE)
                pool.tensor_tensor(w_lo[:, cols], w_sum[:, cols], w_hi[:, cols], ALU.subtract)\
                    .then_inc(s_wl, 1)

            def prepare_pieces(i, r):
                n = 4 * i + r
                add_lora(n, r % 2, 16 * (2 * i + r // 2 + 1))
                if not isinstance(i, int) or n >= 1:
                    high_weights(n - 1)
                if not isinstance(i, int) or n >= 2:
                    low_weights(n - 2)

            pool.wait_ge(s_ones, 5)

            def turn(i):
                for r in range(4):
                    split_max(i, r)
                    if isinstance(i, int) and i == 0 and r == 0:
                        pool.wait_ge(s_vev, CHUNKS)
                        pool.wait_ge(s_lev[0], LORA_KEPT[0])
                        pool.wait_ge(s_lev[1], LORA_KEPT[1])
                    if r % 2 == 0:
                        place_v(i, r // 2)
                    prepare_pieces(i, r)

            turn(0)
            with pool.Fori(1, TURNS) as i:
                turn(i)
            pool.wait_ge(s_wadd, PAIRS)
            high_weights(PAIRS - 1)
            pool.wait_ge(s_wh, PAIRS - 1)
            low_weights(PAIRS - 2)
            pool.wait_ge(s_wh, PAIRS)
            low_weights(PAIRS - 1)

            def norm_o(c):
                for kk in range(DT):
                    pool.wait_ge(s_oc[kk], 32 * (c + 1))
                    pool.tensor_tensor(o_in[:, kk, :], o_in[:, kk, :], den[:, kk, :], ALU.mult).then_inc(s_on, 1)
                    pool.wait_ge(s_oh, DT * c + kk + 1)
                    pool.tensor_tensor(ol[:, kk, :], o_in[:, kk, :], oh[:, kk, :], ALU.subtract).then_inc(s_ol, 1)

            with pool.Fori(1, CHUNKS) as c:
                norm_o(c)

        @block.scalar
        def _(a):
            def std_of(c, stds, count):
                a.wait_ge(count, CT * (c + 1))
                a.activation(std[:, :], mv[:, :, 1], ACT.Sqrt, bias=eps[:, 0:1]).then_inc(stds, 1)

            def keep_turned(i, r):
                pair = r // KT + 1
                if not isinstance(i, int) or 2 * i + pair // 2 > 0:
                    a.wait_ge(s_mrow[pair % 2], 16 * PARTS * (2 * i + pair // 2))
                a.wait_ge(s_mturn, 4 * i + pair + 1)
                a.activation(mturned[pair % 2][:, :], maxslot[0][0:PARTS * MAXUNITS, 0:P // 2].bitcast(BF16),
                             ACT.Copy).then_inc(s_mrows, 1)

            def keep_lora(r):
                for q in range(2):
                    if r == T_STEP - KT and q == 1:
                        keep_turned(0, r)
                    for n in lora_group(r, q):
                        if not by_dve(n):
                            _, _, cols, at0 = lora_tiles[n]
                            a.wait_ge(s_lp, n + 1)
                            a.activation(w_sum[:, at0:at0 + cols], bank[lora_bank(n)][:, 0:cols], ACT.Copy)\
                                .then_inc(s_lev[0], 1)

            a.wait_ge(s_const, 3)
            a.activation(warm[:, 0:1], eps[:, :], ACT.Sqrt)
            std_of(0, s_sd, s_mv)

            def high_rows(c):
                for d in range(DT):
                    a.wait_ge(s_tr, DT * c + d + 1)
                    a.activation(zh[(c + 1) % 2][:, d, :], bank[d], ACT.Copy).then_inc(s_zh, 1)

            a.wait_ge(s_wq, 16)
            for half in (slice(0, 2), slice(2, DT)):
                a.activation(wp_hi[:, half, 0:D], w_raw[:, half, 0:D], ACT.Copy).then_inc(s_whi, 1)
            high_rows(0)
            a.wait_ge(s_wkv, 32)
            a.activation(wp_hi[:, :, D:D + 2 * KVD], w_raw[:, :, D:D + 2 * KVD], ACT.Copy).then_inc(s_whi, 1)
            std_of(1, s_sd, s_mv)
            for c in range(CHUNKS):
                for m in range(5):
                    n = 5 * c + m
                    a.wait_ge(s_proj, 6 * c + m + 1)
                    if n >= 2:
                        done = 3 * c + m // 2 if m % 2 == 0 else 2 * c + m // 2
                        if done:
                            a.wait_ge(s_qst[m % 2], 16 * done)
                    a.activation(qp[m % 2][:, 0, :], bank[(4, 5, 6, 7, 4)[m]], ACT.Copy).then_inc(s_q1, 1)
                    a.wait_ge(s_res, n + 1)
                    a.activation(qp[m % 2][:, 1, :], res[n % 2][:, :], ACT.Copy).then_inc(s_q2, 1)
                    if m == TURN_BEHIND and c + 1 < CHUNKS:
                        high_rows(c + 1)
                    if m == 4 and c + 2 < CHUNKS:
                        std_of(c + 2, s_sd, s_mv)
                if c == CHUNKS - 1:
                    a.wait_ge(s_wo, 2)
                    a.wait_ge(s_wlo, 2)
                    a.wait_ge(s_wlop, 1)
                    a.wait_ge(s_la, 5)
                    for r in TAIL[:CT - 1]:
                        keep_lora(r)
                a.wait_ge(s_proj, 6 * c + 6)
                b, h = c // 2, c % 2
                kept = v_all[:, :].rearrange("p (b k t d) -> p b k t d", b=BATCH, k=KV_HEADS, t=KT)
                a.activation(kept[:, b, :, CT * h:CT * (h + 1), :],
                             bank[5].rearrange("p (t k d) -> p k t d", t=CT, k=KV_HEADS), ACT.Copy)\
                    .then_inc(s_vev, 1)
            a.activation(warm[:, 1:2], eps[:, :], ACT.Exp)
            for r in TAIL[CT - 1:]:
                keep_lora(r)

            def exp_tile(i, r, s):
                t = TURN * i + r
                a.wait_ge(s_score, 4 * t + s + 1)
                if s == 0 and r >= 2:
                    a.wait_ge(s_pv, t - 1)
                a.activation(probs[(r % 2) * 4 + s][:, :], bank[SBANK[s]], ACT.Exp, scale=SCALE)\
                    .then_inc(s_exp, 1)

            def keep_o(i, r):
                a.wait_ge(s_pv, KT * (4 * i + r + 1))
                if not isinstance(i, int) or 2 * i + r // 2 > 0:
                    a.wait_ge(s_od[r % 2], 16 * (2 * i + r // 2))
                a.activation(o_raw[r % 2][:, :], bank[PVBANK], ACT.Copy).then_inc(s_ev, 1)

            def step(i, r):
                if r % KT == 1 and r >= KT:
                    keep_o(i, r // KT - 1)
                for s in range(4):
                    exp_tile(i, r, s)
                if r % KT == T_STEP and not (isinstance(i, int) and i == TURNS - 1 and r > TURN - KT):
                    keep_turned(i, r)

            for r in range(TURN + 2):
                step(0, r)
            with a.Fori(1, TURNS - 1) as i:
                for r in range(2, TURN + 2):
                    step(i, r)
            def turned(c, part, k, i):
                a.wait_ge(s_full, k + 1)
                for q in range(2):
                    a.activation(z2h[:, 2 * part + q, :], slot(i, q), ACT.Copy).then_inc(s_zh2, 1)

            for r in range(2, TURN):
                if r == TURN - 1:
                    turned(0, 0, 2, -2)
                step(TURNS - 1, r)
                if r == STD_STEP:
                    std_of(0, s_sd2, s_mv2)

            def high_o(c, kk):
                n = DT * c + kk
                a.wait_ge(s_on, n + 1)
                a.activation(oh[:, kk, :], o_in[:, kk, :], ACT.Copy).then_inc(s_oh, 1)

            def gate(c, h, k, i):
                n = HT * c + h
                rows = rows_of(h)
                a.wait_ge(s_full, k + 1)
                if not (isinstance(c, int) and c == 0 and h < 2):
                    a.wait_ge(s_hl, n if h == 0 else n - 1)
                a.activation(act[h % 2][0:rows, :], slot(i, 0)[0:rows, :], ACT.Silu).then_inc(s_silu, 1)
                a.wait_ge(s_free, k + 1)
                hidden_read(a, c, h)
                a.activation(hh[h % 2][0:rows, :], act[h % 2][0:rows, :], ACT.Copy).then_inc(s_hh, 1)

            turned(0, 1, 3, -1)
            keep_o(TURNS - 1, 3)

            def chunk(c, last):
                k = 0
                for what, n, i in (LAST_USES if last else USES):
                    at_k = use_index(c, k)
                    if what == "G":
                        gate(c, n, at_k, i)
                        if not last and 1 <= n <= DT:
                            high_o(c + 1, n - 1)
                        if not last and n == 9:
                            std_of(c + 1, s_sd2, s_mv2)
                    if what == "T":
                        turned(c + 1, n, at_k, i)
                    k += 1

            chunk(0, False)
            with a.Fori(1, CHUNKS - 1) as c:
                chunk(c, False)
            chunk(CHUNKS - 1, True)

        @block.vector
        def _(v):
            def stats_of(j, src, loaded, count, stat):
                v.wait_ge(loaded, count)
                v.bn_stats(stats[:, j, :], src[:, j, :]).then_inc(stat, 1)

            def rstd_of(c, stds, rstds):
                v.wait_ge(stds, c + 1)
                v.reciprocal(rstd[:, :], std[:, :]).then_inc(rstds, 1)
                v.wait_ge(rstds, c + 1)

            def mean_var(c):
                for j in range(CT):
                    stats_of(j, xin, s_x[j], 16 * (c + 1), s_st)
                v.wait_ge(s_st, CT * (c + 1))
                for j in range(CT):
                    v.bn_aggr(mv[:, j, :], stats[:, j, :]).then_inc(s_mv, 1)

            def norm(c):
                rstd_of(c, s_sd, s_rs)
                if c:
                    v.wait_ge(s_tr, DT * c)
                for j in range(CT):
                    v.tensor_scalar(z[:, j, :], xin[:, j, :], mv[:, j, 0:1], rstd[:, j:j + 1],
                                    ALU.subtract, ALU.mult).then_inc(s_z, 1)

            def low_rows(c):
                for d in range(DT):
                    v.wait_ge(s_zh, DT * c + d + 1)
                    v.tensor_tensor(zl[(c + 1) % 2][:, d, :], bank[d], zh[(c + 1) % 2][:, d, :], ALU.subtract)\
                        .then_inc(s_zl, 1)

            def max_step(i, r, units):
                for q in units if isinstance(units, range) else range(units):
                    pair, unit = unit_of(r, q) // MAXUNITS, unit_of(r, q) % MAXUNITS
                    if unit == 0 and (pair >= 2 or not isinstance(i, int) or i > 0):
                        v.wait_ge(s_split, 4 * i + pair - 1)
                    v.wait_ge(s_max, TURN_UNITS * i + unit_of(r, q) + 1)
                    v.tensor_reduce(negmax[pair % 2][:, unit:unit + 1], maxslot[q], AX_X, ALU.max,
                                    negate=True).then_inc(s_mred, 1)

            v.memset(kaug[0][QROWS:KROWS, :], 1.0).then_inc(s_ones, 1)
            v.memset(v_cur[0][:, :, :], 1.0).then_inc(s_ones, 1)
            for i in range(2):
                v.memset(mparts[i][:, :], 0.0).then_inc(s_ones, 1)
            v.memset(ones[:, :], 1.0).then_inc(s_ones, 1)
            mean_var(0)
            norm(0)
            for n, half in enumerate((slice(0, 2), slice(2, DT))):
                v.wait_ge(s_whi, n + 1)
                v.tensor_tensor(wp_lo[:, half, 0:D], w_raw[:, half, 0:D], wp_hi[:, half, 0:D], ALU.subtract)\
                    .then_inc(s_wlo, 1)
            low_rows(0)
            mean_var(1)
            norm(1)

            for c in range(CHUNKS):
                for m in range(5):
                    n = 5 * c + m
                    v.wait_ge(s_q1, n + 1)
                    if n >= 2:
                        v.wait_ge(s_q2, n - 1)
                        v.wait_ge(s_q3, n - 1)
                    v.tensor_tensor(res[n % 2][:, :], bank[(4, 5, 6, 7, 4)[m]], qp[m % 2][:, 0, :], ALU.subtract)\
                        .then_inc(s_res, 1)
                    if (c, m) in BESIDE:
                        max_step(0, BESIDE[c, m], range(0, 1))
                    v.wait_ge(s_q2, n + 1)
                    v.tensor_tensor(qp[m % 2][:, 2, :], res[n % 2][:, :], qp[m % 2][:, 1, :], ALU.subtract)\
                        .then_inc(s_q3, 1)
                    if m == MEAN_BEHIND and c + 2 < CHUNKS:
                        mean_var(c + 2)
                    if m == TURN_BEHIND and c + 1 < CHUNKS:
                        low_rows(c + 1)
                    if m == 4 and c + 2 < CHUNKS:
                        norm(c + 2)
                    if (c, m) in BESIDE:
                        max_step(0, BESIDE[c, m], range(1, 2))
                for j in range(CT):
                    if (c, 5 + j) in BESIDE and c < CHUNKS - 1:
                        max_step(0, BESIDE[c, 5 + j], 2)
            v.wait_ge(s_wo, 2)
            v.wait_ge(s_wlop, 1)
            v.wait_ge(s_la, 5)
            for r in TAIL:
                for q in range(2):
                    u = unit_of(r, q)
                    v.wait_ge(s_max, u + 1)
                    v.tensor_reduce(negmax[u // MAXUNITS][:, u % MAXUNITS:u % MAXUNITS + 1], maxslot[q], AX_X,
                                    ALU.max, negate=True).then_inc(s_mred, 1)
                    for n in lora_group(r, q):
                        if by_dve(n):
                            _, _, cols, at0 = lora_tiles[n]
                            v.wait_ge(s_lp, n + 1)
                            v.tensor_copy(w_sum[:, at0:at0 + cols], bank[lora_bank(n)][:, 0:cols])\
                                .then_inc(s_lev[1], 1)

            def units_in(i, r):
                return 2 if i < TURNS - 1 or r < TURN - LEAD else 0

            def invert(i):
                v.wait_ge(s_sum, 16 * (i + 1))
                v.reciprocal(sums[:, :], sums[:, :]).then_inc(s_inv, 1)

            for r in range(TURN):
                max_step(0, r, 2)
            with v.Fori(1, TURNS - 1) as i:
                for r in range(TURN):
                    max_step(i, r, 2)
                    if r == INVERT_STEP:
                        invert(i - 1)
            for r in range(TURN):
                max_step(TURNS - 1, r, units_in(TURNS - 1, r))
                if r == INVERT_STEP:
                    invert(TURNS - 2)

            for kk in range(DT):
                v.wait_ge(s_oc[kk], 32)
                v.tensor_tensor(o_in[:, kk, :], o_in[:, kk, :], den[:, kk, :], ALU.mult).then_inc(s_on, 1)
                v.wait_ge(s_on, kk + 1)
                v.tensor_copy(oh[:, kk, :], o_in[:, kk, :]).then_inc(s_oh, 1)
                v.wait_ge(s_oh, kk + 1)
                v.tensor_tensor(ol[:, kk, :], o_in[:, kk, :], oh[:, kk, :], ALU.subtract).then_inc(s_ol, 1)

            def add_x(c, part, k, i):
                v.wait_ge(s_full, k + 1)
                if part == 0:
                    v.wait_ge(s_xz, 16 * (c + 1))
                else:
                    v.wait_ge(s_st2, CT * c + 2)
                for q in range(2):
                    j = 2 * part + q
                    v.tensor_tensor(xz[:, j, :], slot(i, q), xz[:, j, :], ALU.add)\
                        .then_inc((s_add, s_free)[q], 1)
                if part == 1:
                    mean_of(0)
                stats_of(2 * part, xz, s_add, 2 * c + part + 1, s_st2)
                stats_of(2 * part + 1, xz, s_free, k + 1, s_st2)

            def mean_of(part):
                for j in (2 * part, 2 * part + 1):
                    v.bn_aggr(mv[:, j, :], stats[:, j, :]).then_inc(s_mv2, 1)

            def norm2(c):
                rstd_of(c, s_sd2, s_rs2)
                v.wait_ge(s_x2st, 16 * (c + 1))
                for j in range(CT):
                    v.tensor_scalar(xz[:, j, :], xz[:, j, :], mv[:, j, 0:1], rstd[:, j:j + 1],
                                    ALU.subtract, ALU.mult).then_inc(s_z2, 1)

            def low_turned(c, part, i):
                for q in range(2):
                    v.wait_ge(s_zh2, DT * c + 2 * part + q + 1)
                    low = v.tensor_tensor(z2l[:, 2 * part + q, :], slot(i, q), z2h[:, 2 * part + q, :], ALU.subtract)
                    if q:
                        low.then_inc(s_free, 1)

            def hidden(c, h, k, i, means):
                n = HT * c + h
                rows = rows_of(h)
                if means:
                    v.wait_ge(s_st2, CT * (c + 2))
                v.wait_ge(s_silu, n + 1)
                v.tensor_tensor(act[h % 2][0:rows, :], slot(i, 1)[0:rows, :], act[h % 2][0:rows, :],
                                ALU.mult).then_inc(s_free, 1)
                if means:
                    mean_of(1)
                v.wait_ge(s_hh, n + 1)
                hidden_read(v, c, h)
                v.tensor_tensor(hl[h % 2][0:rows, :], act[h % 2][0:rows, :], hh[h % 2][0:rows, :],
                                ALU.subtract).then_inc(s_hl, 1)

            def add_out(c):
                for j in range(CT):
                    v.wait_ge(s_accr, CT * c + j + 1)
                    v.wait_ge(s_x2l[j], 16 * (c + 1))
                    v.tensor_tensor(x2[j][:, :], bank[j], x2[j][:, :], ALU.add).then_inc(s_acc, 1)

            add_x(0, 0, 0, -2)
            add_x(0, 1, 1, -1)
            v.wait_ge(s_st2, CT)
            mean_of(1)
            norm2(0)
            v.wait_ge(s_score, 4 * STEPS)
            v.wait_ge(s_pv, STEPS - 1)
            for d in (0, 2, 1, 3):
                if d == 1:
                    v.wait_ge(s_pv, STEPS)
                v.wait_ge(s_zh2, d + 1)
                low = v.tensor_tensor(z2l[:, d, :], bank[d], z2h[:, d, :], ALU.subtract)
                if d % 2:
                    low.then_inc(s_free, 1)
            invert(TURNS - 1)

            def chunk(c, last):
                k = 0
                for what, n, i in (LAST_USES if last else USES):
                    at_k = use_index(c, k)
                    if what == "G":
                        hidden(c, n, at_k, i, not last and n == 8)
                        if not last and n == 9:
                            norm2(c + 1)
                    if what == "O":
                        add_x(c + 1, n, at_k, i)
                    if what == "T":
                        low_turned(c + 1, n, i)
                    k += 1
                add_out(c)

            chunk(0, False)
            with v.Fori(1, CHUNKS - 1) as c:
                chunk(c, False)
            chunk(CHUNKS - 1, True)

        @block.tensor
        def _(pe):
            def product(dst, lhs, rhs, first, last, each=False):
                n = len(lhs)
                for t, ((lh, ll), (rh, rl)) in enumerate(zip(lhs, rhs)):
                    if each:
                        pe.wait_ge(s_zl, t + 1)
                    pe.matmul(dst, lh, rh, start=first and t == 0, stop=False)
                    pe.matmul(dst, ll, rh, start=False, stop=False)
                    ins = pe.matmul(dst, lh, rl, start=False, stop=last and t == n - 1)
                return ins

            def turn_rows(c):
                if not isinstance(c, int) or c > 0:
                    pe.wait_ge(s_zl, DT * c)
                for j in range(CT):
                    pe.wait_ge(s_z, CT * c + j + 1)
                    for d in range(DT):
                        ins = pe.transpose(bank[d][:, j * P:(j + 1) * P], z[:, j, d * P:(d + 1) * P],
                                           ident[:, :])
                        if j == CT - 1:
                            ins.then_inc(s_tr, 1)

            def max_unit(i, r, q, half):
                u = unit_of(r, q)
                pair, unit = u // MAXUNITS, u % MAXUNITS
                if unit == 0 and half == 0:
                    pe.wait_ge(s_q[pair % 4], 16 * 6 * (i + pair // 4 + 1))
                    if pair % 2 == 0:
                        pe.wait_ge(s_k[pair // 2 % 2], 16 * 6 * (i + pair // 4 + 1))
                if half == 0 and q == 0 and (r - 1) % KT == T_STEP and r > T_STEP - KT:
                    pe.wait_ge(s_mrows, 4 * i + (r - 1) // KT + 2)
                if half == 0 and (not isinstance(i, int) or TURN_UNITS * i + u >= 2):
                    pe.wait_ge(s_mred, TURN_UNITS * i + u - 1)
                head, qt = unit // KT, unit % KT
                ins = pe.matmul(maxslot[q][:, half * 512:(half + 1) * 512],
                                qaug[pair % 4][0:QROWS, head, qt * P:(qt + 1) * P],
                                kaug[pair // 2 % 2][0:QROWS, half * 512:(half + 1) * 512],
                                start=True, stop=True)
                if half:
                    ins.then_inc(s_max, 1)

            def turn_max(i, r):
                pair = r // KT + 1
                units = unit_of(r, 0) + 1
                if isinstance(i, int):
                    units = min(units, PAIRS * MAXUNITS - TURN_UNITS * i)
                pe.wait_ge(s_split, 4 * i + pair + 1)
                pe.wait_ge(s_mred, TURN_UNITS * i + units)
                pe.transpose(maxslot[0][:, 0:P // 2].bitcast(BF16),
                             mparts[pair % 2][:, :], ident_b[:, :]).then_inc(s_mturn, 1)

            def max_units(r):
                if r == -LEAD:
                    pe.wait_ge(s_zl, DT * CHUNKS)
                if r == TAIL[0]:
                    pe.wait_ge(s_la, 5)
                    pe.wait_ge(s_res, 5 * CHUNKS - 1)
                for q in range(2):
                    for half in range(2):
                        max_unit(0, r, q, half)
                    if r == T_STEP - KT and q == 1:
                        pe.wait_ge(s_ones, 5)
                        turn_max(0, r)
                    for n in lora_group(r, q) if r in TAIL else ():
                        acol, bcol, cols, _ = lora_tiles[n]
                        if n == LORA_EARLY:
                            pe.wait_ge(s_res, 5 * CHUNKS)
                            pe.wait_ge(s_vev, CHUNKS)
                        back = 2 if n < LORA_EARLY else 4
                        if n >= back:
                            pe.wait_ge(*lora_kept(n - back))
                        pe.matmul(bank[lora_bank(n)][:, 0:cols], la[:, acol:acol + P], lb[:, bcol:bcol + cols],
                                  start=True, stop=True).then_inc(s_lp, 1)

            def project(c):
                hi, lo = zh[(c + 1) % 2], zl[(c + 1) % 2]
                if c:
                    pe.wait_ge(s_zl, DT * (c + 1))
                for m in range(5):
                    if m == 0 and c:
                        pe.wait_ge(s_res, 5 * c)
                    if m == 1 and c:
                        pe.wait_ge(s_vev, c)
                    if m in (2, 3) and c:
                        pe.wait_ge(s_res, 5 * c - 4 + m)
                    if m == 4:
                        pe.wait_ge(s_res, 5 * c + 1)
                        pe.wait_ge(s_wlop, 1)
                    w = slice(m * P, (m + 1) * P)
                    product(bank[(4, 5, 6, 7, 4)[m]],
                            [(wp_hi[:, d, w], wp_lo[:, d, w]) for d in range(DT)],
                            [(hi[:, d, :], lo[:, d, :]) for d in range(DT)], True, True,
                            each=c == 0 and m == 0).then_inc(s_proj, 1)
                    if m == TURN_BEHIND and c + 1 < CHUNKS:
                        turn_rows(c + 1)
                    if (c, m) in BESIDE:
                        max_units(BESIDE[c, m])
                pe.wait_ge(s_res, 5 * c + 2)
                w = slice(D + KVD, D + 2 * KVD)
                for j in range(CT):
                    rows = slice(j * P, (j + 1) * P)
                    ins = product(bank[5][:, rows],
                                  [(hi[:, d, rows], lo[:, d, rows]) for d in range(DT)],
                                  [(wp_hi[:, d, w], wp_lo[:, d, w]) for d in range(DT)], True, True)
                    if j == CT - 1:
                        ins.then_inc(s_proj, 1)
                    if (c, 5 + j) in BESIDE:
                        max_units(BESIDE[c, 5 + j])

            pe.wait_ge(s_const, 5)
            turn_rows(0)
            pe.wait_ge(s_wlo, 2)
            for c in range(CHUNKS):
                project(c)

            for r in TAIL[CT:]:
                max_units(r)
            pe.wait_ge(s_ones1, 2)

            def score(i, r, s):
                t = TURN * i + r
                pair, kt = r // KT, r % KT
                if kt == 0 and s == 0:
                    pe.wait_ge(s_mrow[pair % 2], 16 * PARTS * (2 * i + pair // 2 + 1))
                if s == 3:
                    pe.wait_ge(s_exp, 4 * t + 1)
                elif not isinstance(i, int) or t > 0:
                    pe.wait_ge(s_exp, 4 * t - (0, 2, 1)[s])
                head, half = s // 2, s % 2
                pe.matmul(bank[SBANK[s]], kaug[pair // 2 % 2][0:KROWS, kt * P:(kt + 1) * P],
                          qaug[pair % 4][0:KROWS, head, half * CHUNK:(half + 1) * CHUNK],
                          start=True, stop=True).then_inc(s_score, 1)

            def pv(i, r):
                t = TURN * i + r
                pair, kt = r // KT, r % KT
                pe.wait_ge(s_exp, 4 * t + 4)
                if kt == 0:
                    if not isinstance(i, int) or 4 * i + pair > 0:
                        pe.wait_ge(s_ev, 4 * i + pair)
                    pe.wait_ge(s_v, 2 * i + pair // 2 + 1)
                for s in range(4):
                    ins = pe.matmul(bank[PVBANK][32 * s:32 * s + 32, :], v_cur[pair // 2 % 2][:, kt, :],
                                    probs[(r % 2) * 4 + s][:, :], start=kt == 0, stop=kt == KT - 1,
                                    skip_group_check=True)
                ins.then_inc(s_pv, 1)

            def project_first(k):
                t, d = k // DT, k % DT
                rows = slice(t * P, (t + 1) * P)
                if k == 0:
                    pe.wait_ge(s_mred, PAIRS * MAXUNITS)
                    pe.wait_ge(s_mrows, PAIRS)
                    pe.wait_ge(s_wo, 2)
                if t == 0:
                    pe.wait_ge(s_ol, d + 1)
                ins = product(slot(t // 2 - 2, t % 2), [(oh[:, d, rows], ol[:, d, rows])],
                              [(wo_hi[:, d, :], wo_lo[:, d, :])], d == 0, d == DT - 1)
                if t % 2 and d == DT - 1:
                    ins.then_inc(s_full, 1)

            def step(i, r, with_pv=True, units=2, turned=True, pieces=()):
                behind_turn = r % KT == (T_STEP + 1) % KT and r > 0
                for s in range(4):
                    score(i, r, s)
                    if units and not (behind_turn and s == 0):
                        if behind_turn and s == 1:
                            max_unit(i, r, 0, 0)
                        max_unit(i, r, s // 2, s % 2)
                    if s < len(pieces):
                        project_first(pieces[s])
                if with_pv:
                    pv(i, r - 1)
                if r % KT == T_STEP and turned:
                    turn_max(i, r)

            for i in range(2):
                pe.wait_ge(s_lev[i], LORA_KEPT[i])
            for r in range(TURN + 1):
                step(0, r, with_pv=r > 0)
            with pe.Fori(1, TURNS - 1) as i:
                for r in range(1, TURN + 1):
                    step(i, r)
            def free_wait(c, k):
                pe.wait_ge(s_free, use_index(c, 0) if k == 0 else use_index(c, k) - 1)

            def out_project(c, part, i):
                pe.wait_ge(s_ol, DT * (c + 1))
                for q in range(2):
                    rows = slice((2 * part + q) * P, (2 * part + q + 1) * P)
                    ins = product(slot(i, q), [(oh[:, d, rows], ol[:, d, rows]) for d in range(DT)],
                                  [(wo_hi[:, d, :], wo_lo[:, d, :]) for d in range(DT)], True, True)
                ins.then_inc(s_full, 1)

            def turn_rows2(c, part, i):
                pe.wait_ge(s_z2, CT * (c + 1))
                for q in range(2):
                    for j in range(CT):
                        d = 2 * part + q
                        ins = pe.transpose(slot(i, q)[:, j * P:(j + 1) * P], xz[:, j, d * P:(d + 1) * P],
                                           ident[:, :])
                ins.then_inc(s_full, 1)

            def gate_up(c, h, i):
                n = rows_of(h)
                for q, cols in enumerate((gate_w, up_w)):
                    ins = product(slot(i, q)[0:n, :], [(cols(w_hi, d, h, n), cols(w_lo, d, h, n)) for d in range(DT)],
                                  [(z2h[:, d, :], z2l[:, d, :]) for d in range(DT)], True, True)
                ins.then_inc(s_full, 1)

            def down(c, h):
                n = rows_of(h)
                pe.wait_ge(s_hl, HT * c + h + 1)
                if h == 0 and (not isinstance(c, int) or c > 0):
                    pe.wait_ge(s_acc, CT * c)
                for j in range(CT):
                    rows = slice(j * P, (j + 1) * P)
                    ins = product(bank[j], [(hh[h % 2][0:n, rows], hl[h % 2][0:n, rows])],
                                  [(down_w(w_hi, h, n), down_w(w_lo, h, n))], h == 0, h == HT - 1)
                    if h == HT - 1:
                        ins.then_inc(s_accr, 1)
                    elif j == CT - 1:
                        ins.then_inc(s_down, 1)

            for r in range(1, TURN):
                first = O_PIECES * (r - O_STEP)
                step(TURNS - 1, r, units=2 if r < TURN - LEAD else 0, turned=r < TURN - KT,
                     pieces=range(max(0, first), min(CT * DT, first + O_PIECES)))
                if r == T_BEHIND:
                    pe.wait_ge(s_free, 2)
                    turn_rows2(0, 0, -2)
                    turn_rows2(0, 1, -1)
            pv(TURNS - 1, TURN - 1)

            pe.wait_ge(s_exp, 4 * STEPS)
            pe.wait_ge(s_ev, PAIRS)
            pe.wait_ge(s_wl, PAIRS)

            def chunk(c, last):
                k = 0
                for what, n, i in (LAST_USES if last else USES):
                    free_wait(c, k)
                    if what == "G":
                        gate_up(c, n, i)
                        if 0 < n < HT - 1:
                            down(c, n - 1)
                    if what == "O":
                        out_project(c + 1, n, i)
                    if what == "T":
                        turn_rows2(c + 1, n, i)
                        down(c, HT - 2 + n)
                    k += 1
                if last:
                    down(c, HT - 2)
                    down(c, HT - 1)

            chunk(0, False)
            with pe.Fori(1, CHUNKS - 1) as c:
                chunk(c, False)
            chunk(CHUNKS - 1, True)


def kernel(**inputs):
    import numpy as np
    import concourse.bacc as bacc
    from concourse.bass_utils import run_bass_kernel_spmd

    def tiles(w):
        t = -(-w.shape[0] // P)
        full = np.zeros((t * P, w.shape[1]), w.dtype)
        full[:w.shape[0]] = w
        return full.reshape(t, P, w.shape[1]).transpose(1, 0, 2).reshape(P, t * w.shape[1])

    a = {n.replace("L0_attn_", "").replace("L0_ffn_", ""): np.asarray(v) for n, v in inputs.items()}
    down_a = np.zeros((RANK, HT * P), a["down_a"].dtype)
    down_a[:, :FH] = a["down_a"]
    arrays = {
        "x": a["x"].reshape(BATCH * SEQ, D),
        "w_q": a["w_q"], "w_k": a["w_k"], "w_v": a["w_v"], "w_o": a["w_o"],
        "w_ffn": np.concatenate([tiles(a["gate_w"].T), tiles(a["up_w"].T), tiles(a["down_w"].T)], axis=1),
        "lora_a": np.concatenate([a["gate_a"], a["up_a"], down_a], axis=1),
        "lora_b": np.concatenate([a["gate_b"].T, a["up_b"].T, a["down_b"].T], axis=1),
    }
    arrays = {n: np.ascontiguousarray(v) for n, v in arrays.items()}
    nc = bacc.Bacc("TRN2", target_bir_lowering=False, num_devices=1)
    args = [nc.dram_tensor(n, v.shape, mybir.dt.from_np(v.dtype), kind="ExternalInput").ap()
            for n, v in arrays.items()]
    args += [
        nc.dram_tensor("q_parts", (PARTS, BATCH * D, SEQ), BF16).ap(),
        nc.dram_tensor("k_parts", (PARTS, BATCH * KVD, SEQ), BF16).ap(),
        nc.dram_tensor("o_sums", (PAIRS * P, CHUNK), F32).ap(),
        nc.dram_tensor("inverted_sums", (PAIRS * 4, CHUNK), F32).ap(),
        nc.dram_tensor("x_plus_attention", (CHUNKS, P, CT * D), F32).ap(),
        nc.dram_tensor("out", (BATCH * SEQ, D), F32, kind="ExternalOutput").ap(),
    ]
    build(nc, *args)
    r = run_bass_kernel_spmd(nc, [arrays], core_ids=[0])
    return r.results[0]["out"].reshape(BATCH, SEQ, D)
```
